# Optimizing a Trainium2 kernel written in Bass

```python
import numpy as np
import jax
import jax.numpy as jnp

def _softmax(x, axis=-1):
    return jax.nn.softmax(x, axis=axis)

def _gelu(x):
    return jax.nn.gelu(x, approximate=True)

def _silu(x):
    return jax.nn.silu(x)

def _sigmoid(x):
    return jax.nn.sigmoid(x)

def _layernorm(x, axis=-1, eps=1e-05):
    m = jnp.mean(x, axis=axis, keepdims=True)
    v = jnp.var(x, axis=axis, keepdims=True)
    return (x - m) / jnp.sqrt(v + eps)

def _scatter_add(tgt, idx, src, axis=0):
    return tgt.at[idx].add(src)

def _segment_sum(src, seg, n):
    return jax.ops.segment_sum(src, seg, n)
kernel_name = 'mk_prb_d1_jaxref_r8_5cb91b'

def setup_inputs(seed: int=0):
    np.random.seed(seed)
    _w = jnp.asarray

    def _L0_attn_setup():
        import jax, jax.numpy as jnp
        import numpy as np
        NUM_HEADS = 16
        key = jax.random.key(seed)
        ks = jax.random.split(key, 11)
        B, S, D = (4, 128, 128)
        M = 128
        hd = D // NUM_HEADS
        s = 0.02
        return {'x': jax.random.normal(ks[0], (B, S, D), jnp.float32), 'Wq': jax.random.normal(ks[1], (D, D), jnp.float32) * s, 'bq': jax.random.normal(ks[2], (D,), jnp.float32) * s, 'Wk': jax.random.normal(ks[3], (D, D), jnp.float32) * s, 'bk': jax.random.normal(ks[4], (D,), jnp.float32) * s, 'Wv': jax.random.normal(ks[5], (D, D), jnp.float32) * s, 'bv': jax.random.normal(ks[6], (D,), jnp.float32) * s, 'Wo': jax.random.normal(ks[7], (D, D), jnp.float32) * s, 'bo': jax.random.normal(ks[8], (D,), jnp.float32) * s, 'rel_k': jax.random.normal(ks[9], (2 * M + 1, hd), jnp.float32), 'rel_v': jax.random.normal(ks[10], (2 * M + 1, hd), jnp.float32)}
    _L0_attn_in = _L0_attn_setup()

    def _L0_ffn_setup():
        import jax, jax.numpy as jnp
        import numpy as np
        EPS = 1e-05

        def _quantize(W):
            gamma = jnp.mean(jnp.abs(W))
            return jnp.clip(jnp.round(W / (gamma + EPS)), -1.0, 1.0)
        key = jax.random.key(seed)
        k_x, k_w1, k_b1, k_w2, k_b2 = jax.random.split(key, 5)
        n_embd = 128
        d_ff = 4 * n_embd
        B, S = (4, 512)
        bound1 = 1.0 / np.sqrt(n_embd)
        bound2 = 1.0 / np.sqrt(d_ff)
        x = jax.random.normal(k_x, (B, S, n_embd), dtype=jnp.float32)
        W1 = jax.random.uniform(k_w1, (d_ff, n_embd), jnp.float32, -bound1, bound1)
        b1 = jax.random.uniform(k_b1, (d_ff,), jnp.float32, -bound1, bound1)
        W2 = jax.random.uniform(k_w2, (n_embd, d_ff), jnp.float32, -bound2, bound2)
        b2 = jax.random.uniform(k_b2, (n_embd,), jnp.float32, -bound2, bound2)
        return {'x': x, 'W1': W1, 'b1': b1, 'W2': W2, 'b2': b2}
    _L0_ffn_in = _L0_ffn_setup()
    _d = {'L0_attn_x': _L0_attn_in['x'], 'L0_attn_Wq': _L0_attn_in['Wq'], 'L0_attn_bq': _L0_attn_in['bq'], 'L0_attn_Wk': _L0_attn_in['Wk'], 'L0_attn_bk': _L0_attn_in['bk'], 'L0_attn_Wv': _L0_attn_in['Wv'], 'L0_attn_bv': _L0_attn_in['bv'], 'L0_attn_Wo': _L0_attn_in['Wo'], 'L0_attn_bo': _L0_attn_in['bo'], 'L0_attn_rel_k': _L0_attn_in['rel_k'], 'L0_attn_rel_v': _L0_attn_in['rel_v'], 'L0_ffn_W1': _L0_ffn_in['W1'], 'L0_ffn_b1': _L0_ffn_in['b1'], 'L0_ffn_W2': _L0_ffn_in['W2'], 'L0_ffn_b2': _L0_ffn_in['b2']}
    _x0 = _d['L0_attn_x']
    _d['L0_attn_x'] = jax.random.normal(jax.random.fold_in(jax.random.key(seed), 1), (16, 256, 128), dtype=_x0.dtype)
    del _x0
    return _d

def reference(L0_attn_x, L0_attn_Wq, L0_attn_bq, L0_attn_Wk, L0_attn_bk, L0_attn_Wv, L0_attn_bv, L0_attn_Wo, L0_attn_bo, L0_attn_rel_k, L0_attn_rel_v, L0_ffn_W1, L0_ffn_b1, L0_ffn_W2, L0_ffn_b2):

    def _L0_attn_ref(x, Wq, bq, Wk, bk, Wv, bv, Wo, bo, rel_k, rel_v):
        import jax, jax.numpy as jnp
        import numpy as np
        NUM_HEADS = 16
        B, S, D = x.shape
        H = NUM_HEADS
        hd = D // H
        M = (rel_k.shape[0] - 1) // 2

        def proj(W, b):
            return (x @ W.T + b).reshape(B, S, H, hd).transpose(0, 2, 1, 3)
        q = proj(Wq, bq)
        k = proj(Wk, bk)
        v = proj(Wv, bv)
        r = jnp.arange(S)
        idx = jnp.clip(r[None, :] - r[:, None], -M, M) + M
        rpk = rel_k[idx]
        rpv = rel_v[idx]
        content = jnp.einsum('bhqd,bhkd->bhqk', q, k)
        relative = jnp.einsum('bhqd,qkd->bhqk', q, rpk)
        scores = (content + relative) / jnp.sqrt(jnp.float32(hd))
        w = jax.nn.softmax(scores, axis=-1)
        out = jnp.einsum('bhqk,bhkd->bhqd', w, v) + jnp.einsum('bhqk,qkd->bhqd', w, rpv)
        out = out.transpose(0, 2, 1, 3).reshape(B, S, D)
        return out @ Wo.T + bo

    def _L0_ffn_ref(x, W1, b1, W2, b2):
        import jax, jax.numpy as jnp
        import numpy as np
        EPS = 1e-05

        def _quantize(W):
            gamma = jnp.mean(jnp.abs(W))
            return jnp.clip(jnp.round(W / (gamma + EPS)), -1.0, 1.0)
        Wq1 = _quantize(W1)
        Wq2 = _quantize(W2)
        h = jax.nn.relu(jnp.einsum('bsd,fd->bsf', x, Wq1) + b1)
        out = jnp.einsum('bsf,df->bsd', h, Wq2) + b2
        return out
    x = L0_attn_x
    xn = _layernorm(x, axis=-1)
    x = x + _L0_attn_ref(xn, L0_attn_Wq, L0_attn_bq, L0_attn_Wk, L0_attn_bk, L0_attn_Wv, L0_attn_bv, L0_attn_Wo, L0_attn_bo, L0_attn_rel_k, L0_attn_rel_v) + _L0_ffn_ref(xn, L0_ffn_W1, L0_ffn_b1, L0_ffn_W2, L0_ffn_b2)
    return x

_drawn_inputs = setup_inputs


def setup_inputs(seed=0):
    import zlib

    import numpy as np

    out = dict(_drawn_inputs(seed))
    spreads = {}
    factors = {'L0_attn_Wq': 8.0,
     'L0_attn_bq': 8.0,
     'L0_attn_Wk': 8.0,
     'L0_attn_bk': 200.0,
     'L0_attn_Wv': 21.439,
     'L0_attn_bv': 198.814,
     'L0_attn_Wo': 8.0,
     'L0_attn_bo': 200.0,
     'L0_attn_rel_k': 8.0,
     'L0_attn_rel_v': 8.0,
     'L0_ffn_b1': 8.0,
     'L0_ffn_b2': 200.0}
    for name, (base, spread) in spreads.items():
        noise = np.random.default_rng([zlib.crc32(name.encode()), seed]).standard_normal(out[name].shape)
        drawn = base * np.exp(spread * noise) if base else spread * noise
        out[name] = jnp.asarray(drawn.astype(out[name].dtype))
    for name, factor in factors.items():
        out[name] = (out[name] * factor).astype(out[name].dtype)
    return out
```

```python
import math
from contextlib import ExitStack

import numpy as np
import concourse.bass as bass
from concourse import mybir

F32 = mybir.dt.float32
F16 = mybir.dt.float16
BF16 = mybir.dt.bfloat16
ALU = mybir.AluOpType
ACT = mybir.ActivationFunctionType
X_AXIS = mybir.AxisListType.X

B, S, D = 16, 256, 128
H = 16
HD = D // H
M = 128
NREL = 2 * M + 1
FF = 4 * D
P = 128
TOK = B * S
KH = S // P
FT = FF // P
G, HH = 4, 4
PARTS = 3
KR = PARTS * 32
QN = 32
NQB = S // QN
J, Q0 = 4, 8
BG = B // 8
UNITS = B
COLS = H * QN
CH = 4
NCH = TOK // (CH * P)
VC = HH * HD + 1
RC = HD + 1
EW = 2 * S - 1 - 24
ESTART = EW - S
PAD = S - 1 - M
NU = 2 * S - P
LN_EPS = 1e-5
Q_EPS = 1e-5
SCALE = 1.0 / math.sqrt(HD)


def wait(eng, sem, value):
    if isinstance(value, int) and value <= 0:
        return
    eng.wait_ge(sem, value)


def layer_kernel(nc, x, wqT, bq, wkT, bk, wvT, bv, woT, bo, rel_kT, rel_v, w1T, b1, w2T, b2, out):
    ctx = ExitStack()
    with ctx:
        def sb(name, shape, dt):
            return ctx.enter_context(nc.sbuf_tensor(name, shape, dt))

        def sem(name):
            return ctx.enter_context(nc.semaphore(name))

        q_dram = nc.dram_tensor("q_dram", (2, D, TOK), F16, kind="Internal").ap()
        relv_dram = nc.dram_tensor("relv_dram", (2 * S, HD), F32, kind="Internal").ap()
        y_dram = nc.dram_tensor("y_dram", (P, TOK // P, D), F32, kind="Internal").ap()

        wo_sb = sb("wo_sb", [P, D], F32)
        identf = sb("identf", [P, P], F32)
        identb = sb("identb", [P, P], BF16)
        minus1 = sb("minus1", [P, P], BF16)
        sel = sb("sel", [P, QN], F32)
        hmask = sb("hmask", [P, HH], F32)
        kst = sb("kst", [KR, G, TOK], F16)
        e4 = sb("e4", [KR, EW], F16)
        qbd = sb("qbd", [KR, 2, G, HH, J * 8 * Q0], F16)
        qrel = sb("qrel", [KR, 2, H, J, 8 * Q0], F16)
        v_sb = sb("v_sb", [P, TOK // P, G, VC], F32)
        gv = sb("gv", [P, NU, RC], F32)
        attT = sb("attT", [P, B, S], F32)
        xr = sb("xr", [P, BG, S, HD], F32)
        big = sb("big", [P, 2 * 8 * KH * COLS], F32)
        probs = big[:, :].rearrange("p (s k b c) -> p s k b c", s=2, b=8, k=KH)
        at = [0]

        def carve(shape, dt=F32):
            n = int(np.prod(shape)) * (2 if dt == F16 else 4) // 4
            v = big[:, at[0]:at[0] + n]
            at[0] += n
            assert at[0] <= 2 * 8 * KH * COLS
            if dt == F16:
                v = v.bitcast(F16)
            if len(shape) == 1:
                return v
            names = " ".join("abcd"[:len(shape)])
            return v.rearrange(f"p ({names}) -> p {names}", **{c: n for c, n in zip("abcd", shape)})

        x_sb = carve([TOK // P, D])
        xn = carve([2, CH, D])
        xT = carve([2, CH * P])
        hid = carve([FT, CH * P])
        q_hi, q_lo = carve([TOK], F16), carve([TOK], F16)
        k_hi, k_lo = carve([TOK], F16), carve([TOK], F16)
        end_of_first = at[0]
        w1_sb = sb("w1_sb", [P, 2, FF], F32)
        eraw = sb("eraw", [KR, EW], F32)
        gvraw = attT[:, :, :].rearrange("p b s -> p (b s)")[:, 0:NU * HD].rearrange("p (u d) -> p u d", d=HD)
        wqkv = xr[:, 0, :, :].rearrange("p s d -> p (s d)")[:, 0:3 * D].rearrange("p (w n) -> p w n", w=3)
        bvb = xr[:, 0, :, :].rearrange("p s d -> p (s d)")[:, 3 * D:4 * D]
        bobb = xr[:, 0, :, :].rearrange("p s d -> p (s d)")[:, 4 * D:5 * D]
        bo2b = xr[:, 0, :, :].rearrange("p s d -> p (s d)")[:, 5 * D:6 * D]
        onesf = xr[:, 0, :, :].rearrange("p s d -> p (s d)")[:, 6 * D:7 * D]
        bcol = sb("bcol", [P, 2 + FT], F32)
        rcol = sb("rcol", [KR, 2], F32)
        wabs = sb("wabs", [P, 2], F32)
        wdiv = sb("wdiv", [P, 2], F32)
        wthr = sb("wthr", [P, 4], F32)
        wneg = attT[:, :, :].rearrange("p b s -> p (b s)")[:, NU * HD:NU * HD + 2 * FF].rearrange("p (w n) -> p w n", w=2)
        stats = sb("stats", [P, 2, CH, 6], F32)
        mv = sb("mv", [P, 2, CH, 3], F32)
        vare = sb("vare", [P, 2, CH], F32)
        rstd = sb("rstd", [P, 2, CH], F32)
        neghalf = sb("neghalf", [P, CH], F32)
        s0 = sb("s0", [P, 2, COLS], BF16)
        mx = sb("mx", [P, 2, COLS], BF16)
        mcol = sb("mcol", [P, 2, G], F32)
        mdiag = sb("mdiag", [P, G, P], BF16)
        rden = sb("rden", [P, G], F32)
        rmask = sb("rmask", [P, G, HH], F32)
        obd = sb("obd", [P, 2, G, HH, HD], F32)
        rrden = sb("rrden", [P, QN], F32)

        ps_s = ctx.enter_context(nc.psum_tensor("ps_s", [P, 2, KH, COLS], F32))
        ps_t = ctx.enter_context(nc.psum_tensor("ps_t", [P, 512], F32))
        ps_o = ctx.enter_context(nc.psum_tensor("ps_o", [P, 512], F32))
        ps_r = ctx.enter_context(nc.psum_tensor("ps_r", [P, 512], F32))
        ps_y = ctx.enter_context(nc.psum_tensor("ps_y", [P, 512], F32))

        build_first(nc, locals())
        build_main(nc, locals())
        build_last(nc, locals())


def build_first(nc, v):
    x, out = v["x"], v["out"]
    q_dram, relv_dram, y_dram = v["q_dram"], v["relv_dram"], v["y_dram"]
    x_sb, xn, xT, hid = v["x_sb"], v["xn"], v["xT"], v["hid"]
    q_hi, q_lo, k_hi, k_lo = v["q_hi"], v["q_lo"], v["k_hi"], v["k_lo"]
    kst, e4, v_sb, gv, gvraw, eraw = v["kst"], v["e4"], v["v_sb"], v["gv"], v["gvraw"], v["eraw"]
    wqkv, bvb, bobb, bo2b, onesf, bcol = v["wqkv"], v["bvb"], v["bobb"], v["bo2b"], v["onesf"], v["bcol"]
    wthr, wneg = v["wthr"], v["wneg"]
    w1_sb, wabs, wdiv, rcol = v["w1_sb"], v["wabs"], v["wdiv"], v["rcol"]
    stats, mv, vare, rstd, neghalf = v["stats"], v["mv"], v["vare"], v["rstd"], v["neghalf"]
    identf, identb, minus1, sel, hmask = v["identf"], v["identb"], v["minus1"], v["sel"], v["hmask"]
    ps_s, ps_t, ps_o, ps_r, ps_y = v["ps_s"], v["ps_t"], v["ps_o"], v["ps_r"], v["ps_y"]
    ps_f = ps_s[:, 1, 1, :]

    ctx = ExitStack()
    with ctx:
        def sem(name):
            return ctx.enter_context(nc.semaphore(name))

        w_in, ff_in, pad_in = sem("w_in"), sem("ff_in"), sem("pad_in")
        x_in = [sem(f"x_in{i}") for i in range(2)]
        relv_out, gv_in, pads_ready, e_in = sem("relv_out"), sem("gv_in"), sem("pads_ready"), sem("e_in")
        ones_ready, ident_ready, zero_ready = sem("ones_ready"), sem("ident_ready"), sem("zero_ready")
        dve_step = sem("dve_step")
        wabs_ready, gamma_ready, wq_ready = sem("wabs_ready"), sem("gamma_ready"), sem("wq_ready")
        var_ready, rstd_ready, xn_ready = sem("var_ready"), sem("rstd_ready"), sem("xn_ready")
        xnT_ready, xT_ready = sem("xnT_ready"), sem("xT_ready")
        q_ready, k_ready, v_ready = sem("q_ready"), sem("k_ready"), sem("v_ready")
        qhi_ready, khi_ready, qlo_ready, klo_ready = sem("qhi_ready"), sem("khi_ready"), sem("qlo_ready"), sem("klo_ready")
        v_copied, h_ready, hid_ready, f_ready, y_ready = sem("v_copied"), sem("h_ready"), sem("hid_ready"), sem("f_ready"), sem("y_ready")
        y_out = sem("y_out")
        q_out, kst_in = sem("q_out"), sem("kst_in")
        block = ctx.enter_context(nc.Block())

        x_t = x.rearrange("b (h p) d -> p (b h) d", p=P)

        def loop(eng, body):
            body(0, False)
            with eng.Fori(1, NCH // 2 - 1) as i:
                body(i, False)
            body(NCH // 2 - 1, True)

        def tiles(i, p, n=CH):
            return bass.ds(i * (2 * n) + p * n, n)

        @block.sync
        def _(sp):
            half = TOK // P // 2
            sp.dma_start(x_sb[:, 0:half, :], x_t[:, 0:half, :]).then_inc(x_in[0], 16)
            sp.dma_start(wqkv[:, 0, :], v["wqT"]).then_inc(w_in, 16)
            sp.dma_start(wqkv[:, 1, :], v["wkT"]).then_inc(w_in, 16)
            sp.dma_start(wqkv[:, 2, :], v["wvT"]).then_inc(w_in, 16)
            sp.dma_start(bcol[:, 0:1], v["bq"].rearrange("(p o) -> p o", o=1)).then_inc(w_in, 16)
            sp.dma_start(bcol[:, 1:2], v["bk"].rearrange("(p o) -> p o", o=1)).then_inc(w_in, 16)
            with nc.allow_non_contiguous_dma(reason="512 bias values"):
                sp.dma_start(bcol[:, 2:2 + FT], v["b1"].rearrange("(t p) -> p t", p=P)).then_inc(w_in, 16)
            for t, src in ((bvb, "bv"), (bobb, "bo"), (bo2b, "b2")):
                sp.dma_start(t, v[src].rearrange("(o d) -> o d", o=1).to_broadcast([P, D])).then_inc(w_in, 16)
            sp.dma_start(x_sb[:, half:, :], x_t[:, half:, :]).then_inc(x_in[1], 16)
            sp.dma_start(relv_dram[0:PAD, :], v["rel_v"][0:1, :].to_broadcast([PAD, HD])).then_inc(relv_out, 16)
            sp.dma_start(relv_dram[PAD:PAD + NREL, :], v["rel_v"][:, :]).then_inc(relv_out, 16)
            sp.dma_start(relv_dram[PAD + NREL:2 * S, :],
                         v["rel_v"][NREL - 1:NREL, :].to_broadcast([2 * S - PAD - NREL, HD])).then_inc(relv_out, 16)
            sp.wait_ge(relv_out, 48)
            win = bass.AP(tensor=relv_dram.tensor, offset=0, ap=[[HD, P], [1, NU * HD]])
            sp.dma_start(gvraw.rearrange("p u d -> p (u d)"), win).then_inc(gv_in, 16)
            sp.wait_ge(pads_ready, 2)
            for s in range(PARTS):
                for j in range(J):
                    r0, c0 = 32 * s + HD * j, PAD - 24 + 8 * j
                    sp.dma_start(eraw[r0:r0 + HD, c0:c0 + NREL], v["rel_kT"]).then_inc(e_in, 16)

            def body(i, last):
                for p in range(2):
                    sp.wait_ge(y_ready, 2 * i + p + 1)
                    sp.dma_start(y_dram[:, tiles(i, p), :], x_sb[:, tiles(i, p), :]).then_inc(y_out, 16)
            loop(sp, body)
            sp.wait_ge(qlo_ready, NCH)
            for s, src in enumerate((q_hi, q_lo)):
                for bg in range(BG):
                    sp.dma_start(q_dram[s].rearrange("p (a m c) -> a p m c", a=BG, m=NQB * J)[bg],
                                 src.rearrange("p (m a c) -> p m a c", a=BG, m=NQB * J)[:, :, bg, :]).then_inc(q_out, 16)
            sp.wait_ge(klo_ready, NCH)
            for g in range(G):
                for s, src in enumerate((k_hi, k_lo, k_hi)):
                    sp.dma_start(kst[32 * s:32 * s + 32, g, :], src[32 * g:32 * g + 32, :]).then_inc(kst_in, 16)
            sp.wait_ge(y_out, 16 * NCH)
            sp.wait_ge(q_out, 16 * 2 * BG)
            sp.wait_ge(kst_in, 16 * PARTS * G)

        @block.scalar
        def _(act):
            act.dma_start(w1_sb[:, 0, :], v["w1T"]).then_inc(ff_in, 16)
            act.dma_start(w1_sb[:, 1, :].rearrange("p (t n) -> p t n", t=FT),
                          v["w2T"].rearrange("(t p) n -> p t n", p=P)).then_inc(ff_in, 16)
            act.dma_start(v["wo_sb"][:, :], v["woT"]).then_inc(w_in, 16)
            with nc.allow_non_contiguous_dma(reason="end rows of rel_k"):
                for r in range(KR // HD):
                    act.dma_start(rcol[HD * r:HD * r + HD, 0:1], v["rel_kT"][:, 0:1]).then_inc(pad_in, 16)
                    act.dma_start(rcol[HD * r:HD * r + HD, 1:2], v["rel_kT"][:, NREL - 1:NREL]).then_inc(pad_in, 16)

            def copy_xT(c, p):
                wait(act, xnT_ready, c + 1)
                wait(act, f_ready, c - 1)
                nc.scalar.activation(xT[:, p, :], ps_t[:, :], ACT.Copy).then_inc(xT_ready, 1)

            copy_xT(0, 0)
            act.wait_ge(w_in, 160)

            def body(i, last):
                for p in range(2):
                    c = 2 * i + p
                    act.wait_ge(q_ready, c + 1)
                    for b in range(2):
                        dst = q_hi.rearrange("p (m b q) -> p m b q", m=NQB * J, b=B)[:, :, bass.ds(4 * i + 2 * p + b, 1), :]
                        ins = nc.scalar.activation(dst[:, :, 0, :], ps_o[:, S * b:S * b + S].rearrange("p (m q) -> p m q", q=Q0),
                                                   ACT.Identity, bias=bcol[:, 0:1])
                    ins.then_inc(qhi_ready, 1)
                    act.wait_ge(k_ready, c + 1)
                    nc.scalar.activation(k_hi[:, tiles(i, p, CH * P)], ps_r[:, :], ACT.Identity,
                                         bias=bcol[:, 1:2]).then_inc(khi_ready, 1)
                    for f in range(FT):
                        act.wait_ge(h_ready, c * FT + f + 1)
                        wait(act, f_ready, c)
                        nc.scalar.activation(hid[:, f, :], ps_s[:, 0, f % 2, :], ACT.Relu,
                                             bias=bcol[:, 2 + f:3 + f]).then_inc(hid_ready, 1)
                    if not (last and p == 1):
                        copy_xT(c + 1, 1 - p)
            loop(act, body)

        @block.gpsimd
        def _(pool):
            nc.gpsimd.memset(identf[:, :], 0.0).then_inc(zero_ready, 1)
            nc.gpsimd.memset(onesf, 1.0).then_inc(ones_ready, 1)
            nc.gpsimd.memset(neghalf[:, :], -0.5).then_inc(ones_ready, 1)
            pool.wait_ge(zero_ready, 1)
            nc.gpsimd.affine_select(out=identf[:, :], in_=identf[:, :], compare_op=ALU.not_equal, fill=1.0, base=0,
                                    pattern=[[-1, P]], channel_multiplier=1).then_inc(ident_ready, 1)
            pool.wait_ge(ones_ready, 2)

            def inverse_deviation(c, p):
                pool.wait_ge(var_ready, c + 1)
                nc.gpsimd.tensor_tensor(rstd[:, p, :], vare[:, p, :], neghalf[:, :], ALU.pow).then_inc(rstd_ready, 1)

            inverse_deviation(0, 0)

            def body(i, last):
                for p in range(2):
                    if not (last and p == 1):
                        inverse_deviation(2 * i + p + 1, 1 - p)
            loop(pool, body)
            nc.gpsimd.memset(v["qbd"][:, :, :, :, :], 0.0)
            nc.gpsimd.memset(v["qrel"][:, :, :, :, :], 0.0)

        @block.vector
        def _(dve):
            done = [0]

            def step(ins):
                done[0] = done[0] + 1
                ins.then_inc(dve_step, 1)
                dve.wait_ge(dve_step, done[0])

            def norm(i, p, c):
                for t in range(CH):
                    last = nc.vector.bn_stats(stats[:, p, t, :], x_sb[:, bass.ds(i * 2 * CH + p * CH + t, 1), :][:, 0, :])
                step(last)
                st, m = stats[:, p, :, :], mv[:, p, :, :]
                nc.vector.tensor_tensor(m[:, :, 0], st[:, :, 1], st[:, :, 4], ALU.add)
                nc.vector.tensor_tensor(m[:, :, 1], st[:, :, 1], st[:, :, 4], ALU.subtract)
                step(nc.vector.tensor_tensor(m[:, :, 2], st[:, :, 2], st[:, :, 5], ALU.add))
                nc.vector.tensor_scalar(m[:, :, 0], m[:, :, 0], 0.5, None, ALU.mult)
                nc.vector.tensor_scalar(m[:, :, 2], m[:, :, 2], 1.0 / D, LN_EPS, ALU.mult, ALU.add)
                step(nc.vector.tensor_tensor(m[:, :, 1], m[:, :, 1], m[:, :, 1], ALU.mult))
                nc.vector.scalar_tensor_tensor(out=vare[:, p, :], in0=m[:, :, 1], scalar=0.25, in1=m[:, :, 2],
                                               op0=ALU.mult, op1=ALU.add).then_inc(var_ready, 1)
                dve.wait_ge(rstd_ready, c + 1)
                wait(dve, xnT_ready, c - 1)
                for t in range(CH):
                    last = nc.vector.tensor_scalar(xn[:, p, t, :], x_sb[:, bass.ds(i * 2 * CH + p * CH + t, 1), :][:, 0, :],
                                                   mv[:, p, t, 0:1], rstd[:, p, t:t + 1], ALU.subtract, ALU.mult)
                last.then_inc(xn_ready, 1)

            dve.wait_ge(x_in[0], 16)
            norm(0, 0, 0)
            dve.wait_ge(w_in, 160)
            step(nc.vector.tensor_tensor(bo2b, bo2b, bobb, ALU.add))
            dve.wait_ge(ff_in, 32)
            for w in range(2):
                last = nc.vector.tensor_reduce(wabs[:, w:w + 1], w1_sb[:, w, :], X_AXIS, ALU.add,
                                               apply_absolute_value=True)
            last.then_inc(wabs_ready, 1)
            dve.wait_ge(gamma_ready, 1)
            step(nc.vector.tensor_scalar(wdiv[:, :], ps_y[:, 0:2], 1.0 / (FF * D), Q_EPS, ALU.mult, ALU.add))
            step(nc.vector.tensor_scalar(wthr[:, 0:2], wdiv[:, :], 0.5, None, ALU.mult))
            step(nc.vector.tensor_scalar(wthr[:, 2:4], wdiv[:, :], -0.5, None, ALU.mult))
            for w in range(2):
                step(nc.vector.tensor_scalar(wneg[:, w, :], w1_sb[:, w, :], wthr[:, 2 + w:3 + w], None, ALU.is_lt))
            for w in range(2):
                ins = nc.vector.scalar_tensor_tensor(out=w1_sb[:, w, :], in0=w1_sb[:, w, :], scalar=wthr[:, w:w + 1],
                                                     in1=wneg[:, w, :], op0=ALU.is_gt, op1=ALU.subtract)
            ins.then_inc(wq_ready, 1)
            dve.wait_ge(pad_in, 16 * 2 * KR // HD)
            mid = PAD + M
            nc.vector.tensor_copy(eraw[:, 0:mid], rcol[:, 0:1].to_broadcast([KR, mid])).then_inc(pads_ready, 1)
            nc.vector.tensor_copy(eraw[:, mid:], rcol[:, 1:2].to_broadcast([KR, EW - mid])).then_inc(pads_ready, 1)
            dve.wait_ge(ident_ready, 1)
            nc.vector.tensor_copy(identb[:, :], identf[:, :])
            nc.vector.memset(minus1[:, :], -1.0)
            nc.vector.tensor_reduce(sel[:, :], identf[:, :].rearrange("p (h q) -> p q h", h=HH), X_AXIS, ALU.add)
            step(nc.vector.memset(hmask[:, :], 0.0))
            for h in range(HH):
                nc.vector.memset(hmask[32 * h:32 * h + 32, h:h + 1], 1.0)
            nc.vector.memset(v_sb[:, :, :, VC - 1:VC], 1.0)
            nc.vector.memset(gv[:, :, HD:RC], 1.0)
            start = done[0]

            def body(i, last):
                done[0] = start + i * 6
                for p in range(2):
                    c = 2 * i + p
                    if not (last and p == 1):
                        norm(i, 1, c + 1) if p == 0 else norm(i + 1, 0, c + 1)
                    dve.wait_ge(qhi_ready, c + 1)
                    for b in range(2):
                        lo, hi = (t.rearrange("p (m b q) -> p m b q", m=NQB * J, b=B)[:, :, bass.ds(4 * i + 2 * p + b, 1), :][:, :, 0, :]
                                  for t in (q_lo, q_hi))
                        ins = nc.vector.scalar_tensor_tensor(
                            out=lo, in0=ps_o[:, S * b:S * b + S].rearrange("p (m q) -> p m q", q=Q0),
                            scalar=bcol[:, 0:1], in1=hi, op0=ALU.add, op1=ALU.subtract)
                    ins.then_inc(qlo_ready, 1)
                    dve.wait_ge(khi_ready, c + 1)
                    nc.vector.scalar_tensor_tensor(
                        out=k_lo[:, tiles(i, p, CH * P)], in0=ps_r[:, :], scalar=bcol[:, 1:2],
                        in1=k_hi[:, tiles(i, p, CH * P)], op0=ALU.add, op1=ALU.subtract).then_inc(klo_ready, 1)
                    dve.wait_ge(v_ready, c + 1)
                    for t in range(CH):
                        ins = nc.vector.tensor_tensor(
                            v_sb[:, bass.ds(i * 2 * CH + p * CH + t, 1), :, 0:VC - 1][:, 0, :, :],
                            ps_y[:, P * t:P * t + P].rearrange("p (g e) -> p g e", g=G),
                            bvb.rearrange("p (g e) -> p g e", g=G), ALU.add)
                    ins.then_inc(v_copied, 1)
                    dve.wait_ge(f_ready, c + 1)
                    nc.vector.tensor_tensor(x_sb[:, tiles(i, p), :], ps_f.rearrange("p (t n) -> p t n", t=CH),
                                            x_sb[:, tiles(i, p), :], ALU.add).then_inc(y_ready, 1)
            body(0, False)
            dve.wait_ge(x_in[1], 16)
            with dve.Fori(1, NCH // 2 - 1) as i:
                body(i, False)
            body(NCH // 2 - 1, True)
            done[0] = start + 6 * (NCH // 2) - 3
            dve.wait_ge(e_in, 16 * PARTS * J)
            step(nc.vector.tensor_copy(e4[:, :], eraw[:, :]))
            nc.vector.tensor_tensor(e4[32:64, :], eraw[32:64, :], e4[32:64, :], ALU.subtract)
            dve.wait_ge(gv_in, 16)
            nc.vector.tensor_copy(gv[:, :, 0:HD], gvraw)

        @block.tensor
        def _(pe):
            def transpose(c, p):
                pe.wait_ge(xn_ready, c + 1)
                wait(pe, xT_ready, c)
                for t in range(CH):
                    ins = nc.tensor.transpose(ps_t[:, P * t:P * t + P], xn[:, p, t, :], identf[:, :])
                ins.then_inc(xnT_ready, 1)

            pe.wait_ge(ident_ready, 1)
            transpose(0, 0)
            pe.wait_ge(wabs_ready, 1)
            pe.wait_ge(ones_ready, 2)
            nc.tensor.matmul(ps_y[:, 0:2], onesf, wabs[:, :], start=True, stop=True).then_inc(gamma_ready, 1)
            pe.wait_ge(w_in, 160)
            pe.wait_ge(wq_ready, 1)

            def body(i, last):
                for p in range(2):
                    c = 2 * i + p
                    pe.wait_ge(xT_ready, c + 1)
                    wait(pe, qlo_ready, c)
                    nc.tensor.matmul(ps_o[:, :], wqkv[:, 0, :], xT[:, p, :], start=True, stop=True).then_inc(q_ready, 1)
                    wait(pe, klo_ready, c)
                    nc.tensor.matmul(ps_r[:, :], wqkv[:, 1, :], xT[:, p, :], start=True, stop=True).then_inc(k_ready, 1)
                    wait(pe, v_copied, c)
                    for t in range(CH):
                        ins = nc.tensor.matmul(ps_y[:, P * t:P * t + P], xT[:, p, P * t:P * t + P], wqkv[:, 2, :],
                                               start=True, stop=True)
                    ins.then_inc(v_ready, 1)
                    for f in range(FT):
                        wait(pe, hid_ready, c * FT + f - 1)
                        nc.tensor.matmul(ps_s[:, 0, f % 2, :], w1_sb[:, 0, P * f:P * f + P], xT[:, p, :],
                                         start=True, stop=True).then_inc(h_ready, 1)
                    if not (last and p == 1):
                        transpose(c + 1, 1 - p)
                    pe.wait_ge(hid_ready, (c + 1) * FT)
                    wait(pe, y_ready, c)
                    for t in range(CH):
                        for f in range(FT):
                            nc.tensor.matmul(ps_f[:, P * t:P * t + P], hid[:, f, P * t:P * t + P],
                                             w1_sb[:, 1, P * f:P * f + P], start=(f == 0), stop=False)
                        ins = nc.tensor.matmul(ps_f[:, P * t:P * t + P], onesf[0:1, :], bo2b[0:1, :],
                                               start=False, stop=True)
                    ins.then_inc(f_ready, 1)
            loop(pe, body)


def build_main(nc, v):
    q_dram = v["q_dram"]
    kst, e4, qbd, qrel, v_sb, gv, probs = v["kst"], v["e4"], v["qbd"], v["qrel"], v["v_sb"], v["gv"], v["probs"]
    s0 = v["s0"]
    attT, xr, mx, mcol, mdiag = v["attT"], v["xr"], v["mx"], v["mcol"], v["mdiag"]
    rden, rmask, obd, rrden, hmask, sel = v["rden"], v["rmask"], v["obd"], v["rrden"], v["hmask"], v["sel"]
    identb, minus1 = v["identb"], v["minus1"]
    ps_s, ps_o, ps_r, ps_y = v["ps_s"], v["ps_o"], v["ps_r"], v["ps_y"]
    ps_tb = v["ps_t"][:, 0:COLS // 2].bitcast(BF16).rearrange("p (g n) -> p g n", g=G)
    o_ps = ps_o[:, 0:G * VC].rearrange("p (g e) -> p g e", g=G)
    r_ps = ps_r[:, 0:QN * RC].rearrange("p (q e) -> p q e", e=RC)
    y_ps = ps_y[:, 0:8 * QN].rearrange("p (b q) -> p b q", b=8)
    NDMA = 2 * PARTS * 4

    ctx = ExitStack()
    with ctx:
        def sem(name):
            return ctx.enter_context(nc.semaphore(name))

        q_in = [sem(f"q_in{i}") for i in range(2)]
        half_ready, half_copied = sem("half_ready"), sem("half_copied")
        scores_ready, max_ready, maxT_ready = sem("scores_ready"), sem("max_ready"), sem("maxT_ready")
        mcol_ready, mdiag_ready, shifted = sem("mcol_ready"), sem("mdiag_ready"), sem("shifted")
        exp_ready, pv_ready, rden_ready, rmask_ready, obd_ready = sem("exp_ready"), sem("pv_ready"), sem("rden_ready"), sem("rmask_ready"), sem("obd_ready")
        oT_ready, oT_copied = sem("oT_ready"), sem("oT_copied")
        rel_ready, rrden_ready, rel_copied = sem("rel_ready"), sem("rrden_ready"), sem("rel_copied")
        block = ctx.enter_context(nc.Block())

        def loop(eng, body):
            body(0)
            with eng.Fori(1, NQB) as qb:
                body(qb)

        q_src = q_dram.rearrange("s (h d) (a n c) -> s a h d n c", d=HD, a=BG, n=NQB)

        @block.sync
        def _(sp):
            def body(qb):
                for bg in range(BG):
                    su = qb * BG + bg
                    wait(sp, scores_ready, 8 * (su - 1))
                    for s in range(PARTS):
                        part = 1 if s == 2 else 0
                        for k in range(4):
                            src = q_src[part, bg].rearrange("(g k) d n c -> k d g n c", k=HH)[k, :, :, bass.ds(qb, 1), :]
                            sp.dma_start(qbd[32 * s + HD * k:32 * s + HD * k + HD, bg, :, k, :],
                                         src[:, :, 0, :]).then_inc(q_in[bg], 16)
                            src = q_src[part, bg].rearrange("h d n c -> d h n c")[:, :, bass.ds(qb, 1), 64 * k:64 * k + 64]
                            sp.dma_start(qrel[32 * s + HD * k:32 * s + HD * k + HD, bg, :, k, :],
                                         src[:, :, 0, :]).then_inc(q_in[bg], 16)
            loop(sp, body)

        def rel_part(pe, qb, bg, part):
            for q in range(4 * part, 4 * part + 4):
                for kh in range(KH):
                    lhsT = probs[:, bg, kh, :, :].rearrange("p b (h q) -> p (b h) q", q=QN)[:, :, q]
                    win = gv[:, bass.ds(qb * -QN + (P * kh - q + S - 1), 1), :]
                    ins = nc.tensor.matmul(r_ps[:, q, :], lhsT, win[:, 0, :],
                                           start=(q == 0 and kh == 0), stop=(q == QN - 1 and kh == KH - 1),
                                           skip_group_check=True)
            return ins

        @block.tensor
        def _(pe):
            def pv(qb, k):
                n = UNITS * qb + k
                pe.wait_ge(exp_ready, n + 1)
                wait(pe, obd_ready, n)
                for g in range(G):
                    for kh in range(KH):
                        ins = nc.tensor.matmul(o_ps[:, g, :], probs[:, k // 8, kh, k % 8, P * g:P * g + P],
                                               v_sb[:, KH * k + kh, g, :], start=(kh == 0), stop=(kh == KH - 1))
                ins.then_inc(pv_ready, 1)

            def transposed(qb, k):
                n = UNITS * qb + k
                pe.wait_ge(obd_ready, n + 1)
                if k % 8 == 0:
                    wait(pe, oT_copied, BG * qb + k // 8)
                nc.tensor.matmul(y_ps[:, k % 8, :], obd[:, k % 2, :, :, :].rearrange("p g h d -> p (g h d)"), sel[:, :],
                                 start=True, stop=True).then_inc(oT_ready, 1)

            def relative(qb, k, part):
                su = BG * qb + k // 8
                if part == 0:
                    wait(pe, rel_copied, su)
                ins = rel_part(pe, qb, k // 8, part)
                if part == 7:
                    ins.then_inc(rel_ready, 1)

            def body(qb):
                for k in range(UNITS):
                    n = UNITS * qb + k
                    sc = k % 2
                    first = isinstance(qb, int)
                    if k % 8 == 0:
                        pe.wait_ge(q_in[k // 8], (qb + 1) * (16 * NDMA))
                    wait(pe, exp_ready, n - 1)
                    for kh in range(KH):
                        bank = ps_s[:, sc, kh, :]
                        for g in range(G):
                            rhs = qbd[:, k // 8, g, :, :].rearrange("p h (j b q) -> p (h j) b q", j=J, b=8)[:, :, k % 8, :]
                            nc.tensor.matmul(bank[:, P * g:P * g + P],
                                             kst[:, g, S * k + P * kh:S * k + P * kh + P], rhs,
                                             start=(g == 0), stop=False, skip_group_check=True)
                        for q in range(Q0):
                            rhs = qrel[:, k // 8, :, :, :].rearrange("p h j (b q) -> p (h j) b q", b=8)[:, :, k % 8, q]
                            lhsT = e4[:, bass.ds(qb * -QN + (P * kh - q + ESTART), P)]
                            ins = nc.tensor.matmul(bank.rearrange("p (m q) -> p m q", q=Q0)[:, :, q], lhsT, rhs,
                                                   start=False, stop=(q == Q0 - 1), skip_group_check=True)
                        ins.then_inc((half_ready, scores_ready)[kh], 1)
                    if k > 8:
                        relative(qb, 0, k - 9)
                    elif not first:
                        relative(qb - 1, 8 if k else 0, (k - 1) % 8)
                    pe.wait_ge(max_ready, n + 1)
                    wait(pe, mcol_ready, n)
                    for g in range(G):
                        ins = nc.tensor.transpose(ps_tb[:, g, :], mx[:, sc, P * g:P * g + P], identb[:, :])
                    ins.then_inc(maxT_ready, 1)
                    if k > 0:
                        pv(qb, k - 1)
                    elif not first:
                        pv(qb - 1, UNITS - 1)
                    if k > 1:
                        transposed(qb, k - 2)
                    elif not first:
                        transposed(qb - 1, UNITS - 2 + k)
                    pe.wait_ge(mdiag_ready, n + 1)
                    for kh in range(KH):
                        ins = nc.tensor.matmul(ps_s[:, sc, kh, :], minus1[:, :], mdiag[:, :, :].rearrange("p g n -> p (g n)"),
                                               start=False, stop=True, skip_group_check=True)
                    ins.then_inc(shifted, 1)
            loop(pe, body)
            pv(NQB - 1, UNITS - 1)
            transposed(NQB - 1, UNITS - 2)
            transposed(NQB - 1, UNITS - 1)
            relative(NQB - 1, 0, 7)
            for part in range(8):
                relative(NQB - 1, 8, part)

        @block.scalar
        def _(act):
            def copy_oT(qb, bg):
                act.wait_ge(oT_ready, 8 * (BG * qb + bg + 1))
                nc.scalar.activation(attT[:, 8 * bg:8 * bg + 8, bass.ds(qb * QN, QN)], y_ps[:, :, :],
                                     ACT.Copy).then_inc(oT_copied, 1)

            def exponentials(qb, k):
                n = UNITS * qb + k
                act.wait_ge(shifted, n + 1)
                if k % 8 == 0:
                    wait(act, rel_ready, BG * qb + k // 8 - 1)
                nc.scalar.activation(probs[:, k // 8, :, k % 8, :], ps_s[:, k % 2, :, :], ACT.Exp,
                                     scale=SCALE).then_inc(exp_ready, 1)

            def body(qb):
                for k in range(UNITS):
                    n = UNITS * qb + k
                    act.wait_ge(half_ready, n + 1)
                    wait(act, max_ready, n - 1)
                    nc.scalar.activation(s0[:, k % 2, :], ps_s[:, k % 2, 0, :], ACT.Copy).then_inc(half_copied, 1)
                    if k == 10:
                        copy_oT(qb, 0)
                    if k == 2 and not isinstance(qb, int):
                        copy_oT(qb - 1, 1)
                    if k > 0:
                        exponentials(qb, k - 1)
                    elif not isinstance(qb, int):
                        exponentials(qb - 1, UNITS - 1)
            loop(act, body)
            exponentials(NQB - 1, UNITS - 1)
            copy_oT(NQB - 1, 1)

        @block.vector
        def _(dve):
            def mask_outputs(qb, k):
                n = UNITS * qb + k
                dve.wait_ge(pv_ready, n + 1)
                nc.vector.reciprocal(rden[:, :], o_ps[:, :, VC - 1]).then_inc(rden_ready, 1)
                dve.wait_ge(rden_ready, n + 1)
                nc.vector.tensor_tensor(rmask[:, :, :], rden[:, :].rearrange("p (g o) -> p g o", o=1).to_broadcast([P, G, HH]),
                                        hmask[:, :].rearrange("p (o h) -> p o h", o=1).to_broadcast([P, G, HH]),
                                        ALU.mult).then_inc(rmask_ready, 1)
                dve.wait_ge(rmask_ready, n + 1)
                wait(dve, oT_ready, n - 1)
                nc.vector.tensor_tensor(obd[:, k % 2, :, :, :], o_ps[:, :, 0:HH * HD].rearrange("p g (h d) -> p g h d", h=HH),
                                        rmask[:, :, :].rearrange("p g (h o) -> p g h o", o=1).to_broadcast([P, G, HH, HD]),
                                        ALU.mult).then_inc(obd_ready, 1)

            def copy_relative(qb, bg):
                su = BG * qb + bg
                dve.wait_ge(rel_ready, su + 1)
                nc.vector.reciprocal(rrden[:, :], r_ps[:, :, HD]).then_inc(rrden_ready, 1)
                dve.wait_ge(rrden_ready, su + 1)
                nc.vector.tensor_tensor(xr[:, bg, bass.ds(qb * QN, QN), :], r_ps[:, :, 0:HD],
                                        rrden[:, :].rearrange("p (q o) -> p q o", o=1).to_broadcast([P, QN, HD]),
                                        ALU.mult).then_inc(rel_copied, 1)

            def body(qb):
                for k in range(UNITS):
                    n = UNITS * qb + k
                    first = isinstance(qb, int)
                    dve.wait_ge(scores_ready, n + 1)
                    dve.wait_ge(half_copied, n + 1)
                    nc.vector.tensor_tensor(mx[:, k % 2, :], s0[:, k % 2, :], ps_s[:, k % 2, 1, :],
                                            ALU.max).then_inc(max_ready, 1)
                    dve.wait_ge(maxT_ready, n + 1)
                    nc.vector.tensor_reduce(mcol[:, k % 2, :], ps_tb, X_AXIS, ALU.max).then_inc(mcol_ready, 1)
                    dve.wait_ge(mcol_ready, n + 1)
                    wait(dve, shifted, n)
                    nc.vector.tensor_tensor(mdiag[:, :, :], identb[:, :].rearrange("p (o n) -> p o n", o=1).to_broadcast([P, G, P]),
                                            mcol[:, k % 2, :].rearrange("p (g o) -> p g o", o=1).to_broadcast([P, G, P]),
                                            ALU.mult).then_inc(mdiag_ready, 1)
                    if k > 0:
                        mask_outputs(qb, k - 1)
                    elif not first:
                        mask_outputs(qb - 1, UNITS - 1)
                    if k in (0, 8) and not first:
                        copy_relative(qb - 1, k // 8)
            loop(dve, body)
            mask_outputs(NQB - 1, UNITS - 1)
            copy_relative(NQB - 1, 0)
            copy_relative(NQB - 1, 1)


def build_last(nc, v):
    xr, attT, identf, wo_sb, big, y_dram, out = v["xr"], v["attT"], v["identf"], v["wo_sb"], v["big"], v["y_dram"], v["out"]
    ps_s, ps_t, ps_o, ps_r, ps_y = v["ps_s"], v["ps_t"], v["ps_o"], v["ps_r"], v["ps_y"]
    NT = TOK // P
    at = NT * D
    y_sb = big[:, 0:at].rearrange("p (t n) -> p t n", n=D)
    orel = big[:, at:at + 2 * 8 * D].rearrange("p (s b h d) -> p s b h d", s=2, b=8, h=H)
    at += 2 * 8 * D
    oT = big[:, at:at + 2 * 8 * P].rearrange("p (s n) -> p s n", s=2)

    ctx = ExitStack()
    with ctx:
        def sem(name):
            return ctx.enter_context(nc.semaphore(name))

        y_in, d_ready, orel_ready = sem("y_in"), sem("d_ready"), sem("orel_ready")
        relT_ready, oT_ready, out_ready, y_ready, y_out = sem("relT_ready"), sem("oT_sum_ready"), sem("out_ready"), sem("y_sum_ready"), sem("y_sum_out")
        block = ctx.enter_context(nc.Block())
        PARTS_ = [(bg, qh) for bg in range(BG) for qh in range(KH)]
        out_t = out.rearrange("b (h p) d -> h p b d", p=P)
        y_v = y_sb.rearrange("p (b h) d -> p h b d", h=KH)

        @block.sync
        def _(sp):
            sp.dma_start(y_sb, y_dram[:, :, :]).then_inc(y_in, 16)
            for m, (bg, qh) in enumerate(PARTS_):
                sp.wait_ge(y_ready, 2 * (m + 1))
                sp.dma_start(out_t[qh, :, 8 * bg:8 * bg + 8, :], y_v[:, qh, 8 * bg:8 * bg + 8, :]).then_inc(y_out, 16)
            sp.wait_ge(y_out, 16 * len(PARTS_))

        @block.tensor
        def _(pe):
            for m, (bg, qh) in enumerate(PARTS_):
                for half in range(2):
                    wait(pe, orel_ready, 2 * (m - 1) + half + 1)
                    for d in range(4):
                        ins = nc.tensor.transpose(ps_s[:, 0, half, P * d:P * d + P],
                                                  xr[:, bg, P * qh:P * qh + P, 4 * half + d], identf[:, :])
                    ins.then_inc(d_ready, 1)
                pe.wait_ge(orel_ready, 2 * (m + 1))
                for half in range(2):
                    wait(pe, oT_ready, 2 * (m - 1) + half + 1)
                    for b in range(4):
                        ins = nc.tensor.transpose(ps_s[:, 1, half, P * b:P * b + P],
                                                  orel[:, m % 2, 4 * half + b, :, :].rearrange("p h d -> p (h d)"), identf[:, :])
                    ins.then_inc(relT_ready, 1)
                for half in range(2):
                    pe.wait_ge(oT_ready, 2 * m + half + 1)
                    wait(pe, y_ready, 2 * (m - 1) + half + 1)
                    for b in range(4):
                        ins = nc.tensor.matmul((ps_t, ps_o)[half][:, P * b:P * b + P],
                                               oT[:, m % 2, P * (4 * half + b):P * (4 * half + b) + P], wo_sb[:, :],
                                               start=True, stop=True)
                    ins.then_inc(out_ready, 1)

        @block.scalar
        def _(act):
            for m in range(len(PARTS_)):
                for half in range(2):
                    act.wait_ge(d_ready, 2 * m + half + 1)
                    wait(act, relT_ready, 2 * (m - 1))
                    nc.scalar.activation(orel[:, m % 2, :, :, 4 * half:4 * half + 4],
                                         ps_s[:, 0, half, :].rearrange("p (d b h) -> p b h d", d=4, b=8),
                                         ACT.Copy).then_inc(orel_ready, 1)

        @block.vector
        def _(dve):
            dve.wait_ge(y_in, 16)
            for m, (bg, qh) in enumerate(PARTS_):
                for half in range(2):
                    dve.wait_ge(relT_ready, 2 * m + half + 1)
                    b0 = 8 * bg + 4 * half
                    nc.vector.tensor_tensor(oT[:, m % 2, 4 * P * half:4 * P * half + 4 * P].rearrange("p (b q) -> p b q", b=4),
                                            ps_s[:, 1, half, :].rearrange("p (b q) -> p b q", b=4),
                                            attT[:, b0:b0 + 4, P * qh:P * qh + P], ALU.add).then_inc(oT_ready, 1)
                for half in range(2):
                    dve.wait_ge(out_ready, 2 * m + half + 1)
                    b0 = 8 * bg + 4 * half
                    nc.vector.tensor_tensor(y_v[:, qh, b0:b0 + 4, :], (ps_t, ps_o)[half][:, :].rearrange("p (b n) -> p b n", b=4),
                                            y_v[:, qh, b0:b0 + 4, :], ALU.add).then_inc(y_ready, 1)


def kernel(**inputs):
    import concourse.bacc as bacc
    from concourse.bass_utils import run_bass_kernel_spmd

    names = {"L0_attn_x": "x", "L0_attn_Wq": "wqT", "L0_attn_bq": "bq", "L0_attn_Wk": "wkT", "L0_attn_bk": "bk",
             "L0_attn_Wv": "wvT", "L0_attn_bv": "bv", "L0_attn_Wo": "woT", "L0_attn_bo": "bo",
             "L0_attn_rel_k": "rel_kT", "L0_attn_rel_v": "rel_v", "L0_ffn_W1": "w1T", "L0_ffn_b1": "b1",
             "L0_ffn_W2": "w2T", "L0_ffn_b2": "b2"}
    nc = bacc.Bacc("TRN2", target_bir_lowering=False, num_devices=1)
    arrays, args = {}, {}
    for name, short in names.items():
        a = np.asarray(inputs[name])
        a = np.ascontiguousarray(a.T if short.endswith("T") else a)
        arrays[f"in_{short}"] = a
        args[short] = nc.dram_tensor(f"in_{short}", a.shape, mybir.dt.from_np(a.dtype), kind="ExternalInput").ap()
    out = nc.dram_tensor("out", (B, S, D), F32, kind="ExternalOutput").ap()
    layer_kernel(nc, out=out, **args)
    r = run_bass_kernel_spmd(nc, [arrays], core_ids=[0])
    return r.results[0]["out"]
```

```python
import math
from contextlib import ExitStack

import numpy as np
import concourse.bass as bass
from concourse import mybir

F32 = mybir.dt.float32
F16 = mybir.dt.float16
BF16 = mybir.dt.bfloat16
ALU = mybir.AluOpType
ACT = mybir.ActivationFunctionType
X_AXIS = mybir.AxisListType.X

B, S, D = 16, 256, 128
H = 16
HD = D // H
M = 128
NREL = 2 * M + 1
FF = 4 * D
P = 128
TOK = B * S
KH = S // P
FT = FF // P
G, HH = 4, 4
PARTS = 3
KR = PARTS * 32
QN = 32
NQB = S // QN
J, Q0 = 4, 8
BG = B // 8
UNITS = B
COLS = H * QN
CH = 4
NCH = TOK // (CH * P)
VD = HH * HD
VC = 2 * VD + 1
RC = 2 * HD + 1
QH = QN // 2
REL_PARTS = (5, 5, 6, 4, 4, 4, 4)
EW = 2 * S - 1 - 24
ESTART = EW - S
PAD = S - 1 - M
NU = 2 * S - P
LN_EPS = 1e-5
Q_EPS = 1e-5
SCALE = 1.0 / math.sqrt(HD)


def wait(eng, sem, value):
    if isinstance(value, int) and value <= 0:
        return
    eng.wait_ge(sem, value)


def layer_kernel(nc, x, wqT, bq, wkT, bk, wvT, bv, woT, bo, rel_kT, rel_v, w1T, b1, w2T, b2, out):
    ctx = ExitStack()
    with ctx:
        def sb(name, shape, dt):
            return ctx.enter_context(nc.sbuf_tensor(name, shape, dt))

        def sem(name):
            return ctx.enter_context(nc.semaphore(name))

        q_dram = nc.dram_tensor("q_dram", (2, D, TOK), F16, kind="Internal").ap()
        relv_dram = nc.dram_tensor("relv_dram", (2 * S, HD), F32, kind="Internal").ap()
        y_dram = nc.dram_tensor("y_dram", (P, TOK // P, D), F32, kind="Internal").ap()

        wo_sb = sb("wo_sb", [P, D], F32)
        identf = sb("identf", [P, P], F32)
        identb = sb("identb", [P, P], BF16)
        minus1 = sb("minus1", [P, P], BF16)
        sel = sb("sel", [P, QN], F32)
        hmask = sb("hmask", [P, HH], F32)
        kst = sb("kst", [KR, G, TOK], F16)
        e4 = sb("e4", [KR, EW], F16)
        qbd = sb("qbd", [KR, 2, G, HH, J * 8 * Q0], F16)
        qrel = sb("qrel", [KR, 2, H, J, 8 * Q0], F16)
        v_sb = sb("v_sb", [P, TOK // P, G, VC], F16)
        gv = sb("gv", [P, NU, RC], F16)
        attT = sb("attT", [P, B, S], F32)
        xr = sb("xr", [P, BG, S, HD], F32)
        big = sb("big", [P, 2 * 8 * KH * COLS], F32)
        probs = big[:, :].bitcast(F16).rearrange("p (s x k b c) -> p s x k b c", s=2, x=2, b=8, k=KH)
        at = [0]

        def carve(shape, dt=F32):
            n = int(np.prod(shape)) * (2 if dt == F16 else 4) // 4
            v = big[:, at[0]:at[0] + n]
            at[0] += n
            assert at[0] <= 2 * 8 * KH * COLS
            if dt == F16:
                v = v.bitcast(F16)
            if len(shape) == 1:
                return v
            names = " ".join("abcd"[:len(shape)])
            return v.rearrange(f"p ({names}) -> p {names}", **{c: n for c, n in zip("abcd", shape)})

        x_sb = carve([TOK // P, D])
        xn = carve([2, CH, D])
        xT = carve([2, CH * P])
        hid = carve([FT, CH * P])
        q_hi, q_lo = carve([TOK], F16), carve([TOK], F16)
        k_hi, k_lo = carve([TOK], F16), carve([TOK], F16)
        p32 = sb("p32", [P, 2, KH, COLS], F32)
        p32_flat = p32[:, :, :, :].rearrange("p s k c -> p (s k c)")
        w1_sb = p32_flat[:, 0:2 * FF].rearrange("p (w n) -> p w n", w=2)
        v32 = p32_flat[:, 2 * FF:2 * FF + CH * P]
        eraw = p32_flat[0:KR, 2 * FF + CH * P:2 * FF + CH * P + EW]
        gvraw = attT[:, :, :].rearrange("p b s -> p (b s)")[:, 0:NU * HD].rearrange("p (u d) -> p u d", d=HD)
        wqkv = xr[:, 0, :, :].rearrange("p s d -> p (s d)")[:, 0:3 * D].rearrange("p (w n) -> p w n", w=3)
        bvb = xr[:, 0, :, :].rearrange("p s d -> p (s d)")[:, 3 * D:4 * D]
        bobb = xr[:, 0, :, :].rearrange("p s d -> p (s d)")[:, 4 * D:5 * D]
        bo2b = xr[:, 0, :, :].rearrange("p s d -> p (s d)")[:, 5 * D:6 * D]
        onesf = xr[:, 0, :, :].rearrange("p s d -> p (s d)")[:, 6 * D:7 * D]
        bcol = sb("bcol", [P, 2 + FT], F32)
        rcol = sb("rcol", [KR, 2], F32)
        wabs = sb("wabs", [P, 2], F32)
        wdiv = sb("wdiv", [P, 2], F32)
        wthr = sb("wthr", [P, 4], F32)
        wneg = attT[:, :, :].rearrange("p b s -> p (b s)")[:, NU * HD:NU * HD + 2 * FF].rearrange("p (w n) -> p w n", w=2)
        stats = sb("stats", [P, 2, CH, 6], F32)
        mv = sb("mv", [P, 2, CH, 3], F32)
        vare = sb("vare", [P, 2, CH], F32)
        rstd = sb("rstd", [P, 2, CH], F32)
        neghalf = sb("neghalf", [P, CH], F32)
        s0 = sb("s0", [P, 2, COLS], BF16)
        mx = sb("mx", [P, 2, COLS], BF16)
        mcol = sb("mcol", [P, 2, G], F32)
        mdiag = sb("mdiag", [P, G, P], BF16)
        rden = sb("rden", [P, G], F32)
        rmask = sb("rmask", [P, G, HH], F32)
        obd = sb("obd", [P, 2, G, HH, HD], F32)
        rrden = sb("rrden", [P, QH], F32)
        rsum = sb("rsum", [P, QH, HD], F32)

        ps_s = ctx.enter_context(nc.psum_tensor("ps_s", [P, 2, KH, COLS], F32))
        ps_t = ctx.enter_context(nc.psum_tensor("ps_t", [P, 512], F32))
        ps_o = ctx.enter_context(nc.psum_tensor("ps_o", [P, 512], F32))
        ps_r = ctx.enter_context(nc.psum_tensor("ps_r", [P, 512], F32))
        ps_y = ctx.enter_context(nc.psum_tensor("ps_y", [P, 512], F32))

        q_out = [sem(f"q_out{i}") for i in range(BG)]

        build_first(nc, locals())
        build_main(nc, locals())
        build_last(nc, locals())


def build_first(nc, v):
    x, out = v["x"], v["out"]
    q_dram, relv_dram, y_dram = v["q_dram"], v["relv_dram"], v["y_dram"]
    v32 = v["v32"]
    x_sb, xn, xT, hid = v["x_sb"], v["xn"], v["xT"], v["hid"]
    q_hi, q_lo, k_hi, k_lo = v["q_hi"], v["q_lo"], v["k_hi"], v["k_lo"]
    kst, e4, v_sb, gv, gvraw, eraw = v["kst"], v["e4"], v["v_sb"], v["gv"], v["gvraw"], v["eraw"]
    wqkv, bvb, bobb, bo2b, onesf, bcol = v["wqkv"], v["bvb"], v["bobb"], v["bo2b"], v["onesf"], v["bcol"]
    wthr, wneg = v["wthr"], v["wneg"]
    w1_sb, wabs, wdiv, rcol = v["w1_sb"], v["wabs"], v["wdiv"], v["rcol"]
    stats, mv, vare, rstd, neghalf = v["stats"], v["mv"], v["vare"], v["rstd"], v["neghalf"]
    identf, identb, minus1, sel, hmask = v["identf"], v["identb"], v["minus1"], v["sel"], v["hmask"]
    ps_s, ps_t, ps_o, ps_r, ps_y = v["ps_s"], v["ps_t"], v["ps_o"], v["ps_r"], v["ps_y"]
    ps_f = ps_s[:, 1, 1, :]

    ctx = ExitStack()
    with ctx:
        def sem(name):
            return ctx.enter_context(nc.semaphore(name))

        w_in, ff_in, pad_in = sem("w_in"), sem("ff_in"), sem("pad_in")
        x_in = [sem(f"x_in{i}") for i in range(2)]
        relv_out, gv_in, pads_ready, e_in = sem("relv_out"), sem("gv_in"), sem("pads_ready"), sem("e_in")
        ones_ready, ident_ready, zero_ready = sem("ones_ready"), sem("ident_ready"), sem("zero_ready")
        dve_step = sem("dve_step")
        wabs_ready, gamma_ready, wq_ready = sem("wabs_ready"), sem("gamma_ready"), sem("wq_ready")
        var_ready, rstd_ready, xn_ready = sem("var_ready"), sem("rstd_ready"), sem("xn_ready")
        xnT_ready, xT_ready = sem("xnT_ready"), sem("xT_ready")
        q_ready, k_ready, v_ready = sem("q_ready"), sem("k_ready"), sem("v_ready")
        qhi_ready, khi_ready, qlo_ready, klo_ready = sem("qhi_ready"), sem("khi_ready"), sem("qlo_ready"), sem("klo_ready")
        v32_ready, v_copied, h_ready, hid_ready, f_ready, y_ready = sem("v32_ready"), sem("v_copied"), sem("h_ready"), sem("hid_ready"), sem("f_ready"), sem("y_ready")
        y_out = sem("y_out")
        kst_in = sem("kst_in")
        q_out = v["q_out"]
        block = ctx.enter_context(nc.Block())

        x_t = x.rearrange("b (h p) d -> p (b h) d", p=P)

        def loop(eng, body):
            body(0, False)
            with eng.Fori(1, NCH // 2 - 1) as i:
                body(i, False)
            body(NCH // 2 - 1, True)

        def tiles(i, p, n=CH):
            return bass.ds(i * (2 * n) + p * n, n)

        @block.sync
        def _(sp):
            half = TOK // P // 2
            sp.dma_start(x_sb[:, 0:half, :], x_t[:, 0:half, :]).then_inc(x_in[0], 16)
            sp.dma_start(wqkv[:, 0, :], v["wqT"]).then_inc(w_in, 16)
            sp.dma_start(wqkv[:, 1, :], v["wkT"]).then_inc(w_in, 16)
            sp.dma_start(wqkv[:, 2, :], v["wvT"]).then_inc(w_in, 16)
            sp.dma_start(bcol[:, 0:1], v["bq"].rearrange("(p o) -> p o", o=1)).then_inc(w_in, 16)
            sp.dma_start(bcol[:, 1:2], v["bk"].rearrange("(p o) -> p o", o=1)).then_inc(w_in, 16)
            with nc.allow_non_contiguous_dma(reason="512 bias values"):
                sp.dma_start(bcol[:, 2:2 + FT], v["b1"].rearrange("(t p) -> p t", p=P)).then_inc(w_in, 16)
            for t, src in ((bvb, "bv"), (bobb, "bo"), (bo2b, "b2")):
                sp.dma_start(t, v[src].rearrange("(o d) -> o d", o=1).to_broadcast([P, D])).then_inc(w_in, 16)
            sp.dma_start(x_sb[:, half:, :], x_t[:, half:, :]).then_inc(x_in[1], 16)
            sp.dma_start(relv_dram[0:PAD, :], v["rel_v"][0:1, :].to_broadcast([PAD, HD])).then_inc(relv_out, 16)
            sp.dma_start(relv_dram[PAD:PAD + NREL, :], v["rel_v"][:, :]).then_inc(relv_out, 16)
            sp.dma_start(relv_dram[PAD + NREL:2 * S, :],
                         v["rel_v"][NREL - 1:NREL, :].to_broadcast([2 * S - PAD - NREL, HD])).then_inc(relv_out, 16)
            sp.wait_ge(relv_out, 48)
            win = bass.AP(tensor=relv_dram.tensor, offset=0, ap=[[HD, P], [1, NU * HD]])
            sp.dma_start(gvraw.rearrange("p u d -> p (u d)"), win).then_inc(gv_in, 16)
            sp.wait_ge(pads_ready, 2)
            for s in range(PARTS):
                for j in range(J):
                    r0, c0 = 32 * s + HD * j, PAD - 24 + 8 * j
                    sp.dma_start(eraw[r0:r0 + HD, c0:c0 + NREL], v["rel_kT"]).then_inc(e_in, 16)

            def body(i, last):
                for p in range(2):
                    c = 2 * i + p
                    sp.wait_ge(klo_ready, c + 1)
                    for g in range(G):
                        for s, src in enumerate((k_hi, k_lo, k_hi)):
                            sp.dma_start(kst[32 * s:32 * s + 32, g, tiles(i, p, CH * P)],
                                         src[32 * g:32 * g + 32, tiles(i, p, CH * P)]).then_inc(kst_in, 16)
                    sp.wait_ge(y_ready, c + 1)
                    sp.dma_start(y_dram[:, tiles(i, p), :], x_sb[:, tiles(i, p), :]).then_inc(y_out, 16)
            loop(sp, body)
            sp.wait_ge(y_out, 16 * NCH)
            sp.wait_ge(kst_in, 16 * PARTS * G * NCH)

        @block.scalar
        def _(act):
            act.dma_start(w1_sb[:, 0, :], v["w1T"]).then_inc(ff_in, 16)
            act.dma_start(w1_sb[:, 1, :].rearrange("p (t n) -> p t n", t=FT),
                          v["w2T"].rearrange("(t p) n -> p t n", p=P)).then_inc(ff_in, 16)
            act.dma_start(v["wo_sb"][:, :], v["woT"]).then_inc(w_in, 16)
            with nc.allow_non_contiguous_dma(reason="end rows of rel_k"):
                for r in range(KR // HD):
                    act.dma_start(rcol[HD * r:HD * r + HD, 0:1], v["rel_kT"][:, 0:1]).then_inc(pad_in, 16)
                    act.dma_start(rcol[HD * r:HD * r + HD, 1:2], v["rel_kT"][:, NREL - 1:NREL]).then_inc(pad_in, 16)

            def copy_xT(c, p):
                wait(act, xnT_ready, c + 1)
                wait(act, f_ready, c - 1)
                nc.scalar.activation(xT[:, p, :], ps_t[:, :], ACT.Copy).then_inc(xT_ready, 1)

            copy_xT(0, 0)
            act.wait_ge(w_in, 160)

            def body(i, last):
                for p in range(2):
                    c = 2 * i + p
                    act.wait_ge(q_ready, c + 1)
                    for b in range(2):
                        dst = q_hi.rearrange("p (m b q) -> p m b q", m=NQB * J, b=B)[:, :, bass.ds(4 * i + 2 * p + b, 1), :]
                        ins = nc.scalar.activation(dst[:, :, 0, :], ps_o[:, S * b:S * b + S].rearrange("p (m q) -> p m q", q=Q0),
                                                   ACT.Identity, bias=bcol[:, 0:1])
                    ins.then_inc(qhi_ready, 1)
                    act.wait_ge(k_ready, c + 1)
                    nc.scalar.activation(k_hi[:, tiles(i, p, CH * P)], ps_r[:, :], ACT.Identity,
                                         bias=bcol[:, 1:2]).then_inc(khi_ready, 1)
                    for f in range(FT):
                        act.wait_ge(h_ready, c * FT + f + 1)
                        wait(act, f_ready, c)
                        nc.scalar.activation(hid[:, f, :], ps_s[:, 0, f % 2, :], ACT.Relu,
                                             bias=bcol[:, 2 + f:3 + f]).then_inc(hid_ready, 1)
                    if not (last and p == 1):
                        copy_xT(c + 1, 1 - p)
            loop(act, body)

        @block.gpsimd
        def _(pool):
            nc.gpsimd.memset(identf[:, :], 0.0).then_inc(zero_ready, 1)
            nc.gpsimd.memset(onesf, 1.0).then_inc(ones_ready, 1)
            nc.gpsimd.memset(neghalf[:, :], -0.5).then_inc(ones_ready, 1)
            pool.wait_ge(zero_ready, 1)
            nc.gpsimd.affine_select(out=identf[:, :], in_=identf[:, :], compare_op=ALU.not_equal, fill=1.0, base=0,
                                    pattern=[[-1, P]], channel_multiplier=1).then_inc(ident_ready, 1)
            pool.wait_ge(ones_ready, 2)

            def inverse_deviation(c, p):
                pool.wait_ge(var_ready, c + 1)
                nc.gpsimd.tensor_tensor(rstd[:, p, :], vare[:, p, :], neghalf[:, :], ALU.pow).then_inc(rstd_ready, 1)

            inverse_deviation(0, 0)
            nc.gpsimd.memset(v["qbd"][:, :, :, :, :], 0.0)
            nc.gpsimd.memset(v["qrel"][:, :, :, :, :], 0.0)

            def body(i, last):
                for p in range(2):
                    if not (last and p == 1):
                        inverse_deviation(2 * i + p + 1, 1 - p)
            loop(pool, body)
            for bg in range(BG):
                pool.wait_ge(qlo_ready, NCH // 2 * (bg + 1))
                for s, src in enumerate((q_hi, q_lo)):
                    pool.dma_start(q_dram[s].rearrange("p (a m c) -> a p m c", a=BG, m=NQB * J)[bg],
                                   src.rearrange("p (m a c) -> p m a c", a=BG, m=NQB * J)[:, :, bg, :]).then_inc(q_out[bg], 16)

        @block.vector
        def _(dve):
            done = [0]

            def step(ins):
                done[0] = done[0] + 1
                ins.then_inc(dve_step, 1)
                dve.wait_ge(dve_step, done[0])

            def norm(i, p, c):
                for t in range(CH):
                    last = nc.vector.bn_stats(stats[:, p, t, :], x_sb[:, bass.ds(i * 2 * CH + p * CH + t, 1), :][:, 0, :])
                step(last)
                st, m = stats[:, p, :, :], mv[:, p, :, :]
                nc.vector.tensor_tensor(m[:, :, 0], st[:, :, 1], st[:, :, 4], ALU.add)
                nc.vector.tensor_tensor(m[:, :, 1], st[:, :, 1], st[:, :, 4], ALU.subtract)
                step(nc.vector.tensor_tensor(m[:, :, 2], st[:, :, 2], st[:, :, 5], ALU.add))
                nc.vector.tensor_scalar(m[:, :, 0], m[:, :, 0], 0.5, None, ALU.mult)
                nc.vector.tensor_scalar(m[:, :, 2], m[:, :, 2], 1.0 / D, LN_EPS, ALU.mult, ALU.add)
                step(nc.vector.tensor_tensor(m[:, :, 1], m[:, :, 1], m[:, :, 1], ALU.mult))
                nc.vector.scalar_tensor_tensor(out=vare[:, p, :], in0=m[:, :, 1], scalar=0.25, in1=m[:, :, 2],
                                               op0=ALU.mult, op1=ALU.add).then_inc(var_ready, 1)
                dve.wait_ge(rstd_ready, c + 1)
                wait(dve, xnT_ready, c - 1)
                for t in range(CH):
                    last = nc.vector.tensor_scalar(xn[:, p, t, :], x_sb[:, bass.ds(i * 2 * CH + p * CH + t, 1), :][:, 0, :],
                                                   mv[:, p, t, 0:1], rstd[:, p, t:t + 1], ALU.subtract, ALU.mult)
                last.then_inc(xn_ready, 1)

            dve.wait_ge(x_in[0], 16)
            norm(0, 0, 0)
            dve.wait_ge(w_in, 160)
            step(nc.vector.tensor_tensor(bo2b, bo2b, bobb, ALU.add))
            dve.wait_ge(ff_in, 32)
            for w in range(2):
                last = nc.vector.tensor_reduce(wabs[:, w:w + 1], w1_sb[:, w, :], X_AXIS, ALU.add,
                                               apply_absolute_value=True)
            last.then_inc(wabs_ready, 1)
            dve.wait_ge(gamma_ready, 1)
            step(nc.vector.tensor_scalar(wdiv[:, :], ps_y[:, 0:2], 1.0 / (FF * D), Q_EPS, ALU.mult, ALU.add))
            step(nc.vector.tensor_scalar(wthr[:, 0:2], wdiv[:, :], 0.5, None, ALU.mult))
            step(nc.vector.tensor_scalar(wthr[:, 2:4], wdiv[:, :], -0.5, None, ALU.mult))
            for w in range(2):
                step(nc.vector.tensor_scalar(wneg[:, w, :], w1_sb[:, w, :], wthr[:, 2 + w:3 + w], None, ALU.is_lt))
            for w in range(2):
                ins = nc.vector.scalar_tensor_tensor(out=w1_sb[:, w, :], in0=w1_sb[:, w, :], scalar=wthr[:, w:w + 1],
                                                     in1=wneg[:, w, :], op0=ALU.is_gt, op1=ALU.subtract)
            ins.then_inc(wq_ready, 1)
            dve.wait_ge(pad_in, 16 * 2 * KR // HD)
            mid = PAD + M
            nc.vector.tensor_copy(eraw[:, 0:mid], rcol[:, 0:1].to_broadcast([KR, mid])).then_inc(pads_ready, 1)
            nc.vector.tensor_copy(eraw[:, mid:], rcol[:, 1:2].to_broadcast([KR, EW - mid])).then_inc(pads_ready, 1)
            dve.wait_ge(ident_ready, 1)
            nc.vector.tensor_copy(identb[:, :], identf[:, :])
            nc.vector.memset(minus1[:, :], -1.0)
            nc.vector.tensor_reduce(sel[:, :], identf[:, :].rearrange("p (h q) -> p q h", h=HH), X_AXIS, ALU.add)
            step(nc.vector.memset(hmask[:, :], 0.0))
            for h in range(HH):
                nc.vector.memset(hmask[32 * h:32 * h + 32, h:h + 1], 1.0)
            nc.vector.memset(v_sb[:, :, :, VD:VD + 1], 1.0)
            nc.vector.memset(gv[:, :, HD:HD + 1], 1.0)
            start = done[0]

            def body(i, last):
                done[0] = start + i * 6
                for p in range(2):
                    c = 2 * i + p
                    if not (last and p == 1):
                        norm(i, 1, c + 1) if p == 0 else norm(i + 1, 0, c + 1)
                    dve.wait_ge(qhi_ready, c + 1)
                    for b in range(2):
                        lo, hi = (t.rearrange("p (m b q) -> p m b q", m=NQB * J, b=B)[:, :, bass.ds(4 * i + 2 * p + b, 1), :][:, :, 0, :]
                                  for t in (q_lo, q_hi))
                        ins = nc.vector.scalar_tensor_tensor(
                            out=lo, in0=ps_o[:, S * b:S * b + S].rearrange("p (m q) -> p m q", q=Q0),
                            scalar=bcol[:, 0:1], in1=hi, op0=ALU.add, op1=ALU.subtract)
                    ins.then_inc(qlo_ready, 1)
                    dve.wait_ge(khi_ready, c + 1)
                    nc.vector.scalar_tensor_tensor(
                        out=k_lo[:, tiles(i, p, CH * P)], in0=ps_r[:, :], scalar=bcol[:, 1:2],
                        in1=k_hi[:, tiles(i, p, CH * P)], op0=ALU.add, op1=ALU.subtract).then_inc(klo_ready, 1)
                    dve.wait_ge(v_ready, c + 1)
                    wait(dve, v_copied, 2 * c)
                    nc.vector.tensor_tensor(v32.rearrange("p (t n) -> p t n", t=CH), ps_y[:, :].rearrange("p (t n) -> p t n", t=CH),
                                            bvb.rearrange("p (o n) -> p o n", o=1).to_broadcast([P, CH, D]),
                                            ALU.add).then_inc(v32_ready, 1)
                    dve.wait_ge(v32_ready, c + 1)
                    v4 = v32.rearrange("p (t g e) -> p t g e", t=CH, g=G)
                    v_hi = v_sb[:, tiles(i, p), :, 0:VD]
                    nc.vector.tensor_copy(v_hi, v4).then_inc(v_copied, 1)
                    dve.wait_ge(v_copied, 2 * c + 1)
                    nc.vector.tensor_tensor(v_sb[:, tiles(i, p), :, VD + 1:VC], v4, v_hi,
                                            ALU.subtract).then_inc(v_copied, 1)
                    dve.wait_ge(f_ready, c + 1)
                    nc.vector.tensor_tensor(x_sb[:, tiles(i, p), :], ps_f.rearrange("p (t n) -> p t n", t=CH),
                                            x_sb[:, tiles(i, p), :], ALU.add).then_inc(y_ready, 1)
            body(0, False)
            dve.wait_ge(x_in[1], 16)
            with dve.Fori(1, NCH // 2 - 1) as i:
                body(i, False)
            body(NCH // 2 - 1, True)
            done[0] = start + 6 * (NCH // 2) - 3
            dve.wait_ge(e_in, 16 * PARTS * J)
            step(nc.vector.tensor_copy(e4[:, :], eraw[:, :]))
            nc.vector.tensor_tensor(e4[32:64, :], eraw[32:64, :], e4[32:64, :], ALU.subtract)
            dve.wait_ge(gv_in, 16)
            step(nc.vector.tensor_copy(gv[:, :, 0:HD], gvraw))
            nc.vector.tensor_tensor(gv[:, :, HD + 1:RC], gvraw, gv[:, :, 0:HD], ALU.subtract)

        @block.tensor
        def _(pe):
            def transpose(c, p):
                pe.wait_ge(xn_ready, c + 1)
                wait(pe, xT_ready, c)
                for t in range(CH):
                    ins = nc.tensor.transpose(ps_t[:, P * t:P * t + P], xn[:, p, t, :], identf[:, :])
                ins.then_inc(xnT_ready, 1)

            pe.wait_ge(ident_ready, 1)
            transpose(0, 0)
            pe.wait_ge(wabs_ready, 1)
            pe.wait_ge(ones_ready, 2)
            nc.tensor.matmul(ps_y[:, 0:2], onesf, wabs[:, :], start=True, stop=True).then_inc(gamma_ready, 1)
            pe.wait_ge(w_in, 160)
            pe.wait_ge(wq_ready, 1)

            def body(i, last):
                for p in range(2):
                    c = 2 * i + p
                    pe.wait_ge(xT_ready, c + 1)
                    wait(pe, qlo_ready, c)
                    nc.tensor.matmul(ps_o[:, :], wqkv[:, 0, :], xT[:, p, :], start=True, stop=True).then_inc(q_ready, 1)
                    wait(pe, klo_ready, c)
                    nc.tensor.matmul(ps_r[:, :], wqkv[:, 1, :], xT[:, p, :], start=True, stop=True).then_inc(k_ready, 1)
                    wait(pe, v32_ready, c)
                    for t in range(CH):
                        ins = nc.tensor.matmul(ps_y[:, P * t:P * t + P], xT[:, p, P * t:P * t + P], wqkv[:, 2, :],
                                               start=True, stop=True)
                    ins.then_inc(v_ready, 1)
                    for f in range(FT):
                        wait(pe, hid_ready, c * FT + f - 1)
                        nc.tensor.matmul(ps_s[:, 0, f % 2, :], w1_sb[:, 0, P * f:P * f + P], xT[:, p, :],
                                         start=True, stop=True).then_inc(h_ready, 1)
                    if not (last and p == 1):
                        transpose(c + 1, 1 - p)
                    pe.wait_ge(hid_ready, (c + 1) * FT)
                    wait(pe, y_ready, c)
                    for t in range(CH):
                        for f in range(FT):
                            nc.tensor.matmul(ps_f[:, P * t:P * t + P], hid[:, f, P * t:P * t + P],
                                             w1_sb[:, 1, P * f:P * f + P], start=(f == 0), stop=False)
                        ins = nc.tensor.matmul(ps_f[:, P * t:P * t + P], onesf[0:1, :], bo2b[0:1, :],
                                               start=False, stop=True)
                    ins.then_inc(f_ready, 1)
            loop(pe, body)


def build_main(nc, v):
    q_dram, q_out = v["q_dram"], v["q_out"]
    kst, e4, qbd, qrel, v_sb, gv, probs = v["kst"], v["e4"], v["qbd"], v["qrel"], v["v_sb"], v["gv"], v["probs"]
    s0, p32, rsum = v["s0"], v["p32"], v["rsum"]
    attT, xr, mx, mcol, mdiag = v["attT"], v["xr"], v["mx"], v["mcol"], v["mdiag"]
    rden, rmask, obd, rrden, hmask, sel = v["rden"], v["rmask"], v["obd"], v["rrden"], v["hmask"], v["sel"]
    identb, minus1 = v["identb"], v["minus1"]
    ps_s, ps_o, ps_r, ps_y = v["ps_s"], v["ps_o"], v["ps_r"], v["ps_y"]
    ps_tb = v["ps_t"][:, 0:COLS // 2].bitcast(BF16).rearrange("p (g n) -> p g n", g=G)
    o_ps = ps_o[:, 0:G * (VD + 1)].rearrange("p (g e) -> p g e", g=G)
    r_ps = ps_r[:, 0:QH * RC].rearrange("p (q e) -> p q e", e=RC)
    y_ps = ps_y[:, 0:8 * QN].rearrange("p (b q) -> p b q", b=8)
    NDMA = 2 * PARTS * 4

    ctx = ExitStack()
    with ctx:
        def sem(name):
            return ctx.enter_context(nc.semaphore(name))

        q_in = [sem(f"q_in{i}") for i in range(2)]
        half_ready, half_copied = sem("half_ready"), sem("half_copied")
        scores_ready, max_ready, maxT_ready = sem("scores_ready"), sem("max_ready"), sem("maxT_ready")
        mcol_ready, mdiag_ready, shifted = sem("mcol_ready"), sem("mdiag_ready"), sem("shifted")
        hi_ready, lo_ready, pool_lo_ready = sem("hi_ready"), sem("lo_ready"), sem("pool_lo_ready")
        rsum_ready = sem("rsum_ready")
        exp_ready, pv_ready, rden_ready, rmask_ready, obd_ready = sem("exp_ready"), sem("pv_ready"), sem("rden_ready"), sem("rmask_ready"), sem("obd_ready")
        oT_ready, oT_copied = sem("oT_ready"), sem("oT_copied")
        rel_ready, rrden_ready, rel_copied = sem("rel_ready"), sem("rrden_ready"), sem("rel_copied")
        block = ctx.enter_context(nc.Block())

        def loop(eng, body):
            body(0, False)
            with eng.Fori(1, NQB - 1) as qb:
                body(qb, False)
            body(NQB - 1, True)

        def unit(qb, k):
            if k < 0 and isinstance(qb, int) and qb == 0:
                return None
            return (qb - 1, k + UNITS) if k < 0 else (qb, k)

        q_src = q_dram.rearrange("s (h d) (a n c) -> s a h d n c", d=HD, a=BG, n=NQB)

        @block.sync
        def _(sp):
            def body(qb, last):
                for bg in range(BG):
                    su = qb * BG + bg
                    if isinstance(qb, int) and qb == 0:
                        sp.wait_ge(q_out[bg], 32)
                    wait(sp, scores_ready, 8 * (su - 1))
                    for s in range(PARTS):
                        part = 1 if s == 2 else 0
                        for k in range(4):
                            src = q_src[part, bg].rearrange("(g k) d n c -> k d g n c", k=HH)[k, :, :, bass.ds(qb, 1), :]
                            sp.dma_start(qbd[32 * s + HD * k:32 * s + HD * k + HD, bg, :, k, :],
                                         src[:, :, 0, :]).then_inc(q_in[bg], 16)
                            src = q_src[part, bg].rearrange("h d n c -> d h n c")[:, :, bass.ds(qb, 1), 64 * k:64 * k + 64]
                            sp.dma_start(qrel[32 * s + HD * k:32 * s + HD * k + HD, bg, :, k, :],
                                         src[:, :, 0, :]).then_inc(q_in[bg], 16)
            loop(sp, body)

        @block.tensor
        def _(pe):
            def scores(qb, k):
                if k % 8 == 0:
                    pe.wait_ge(q_in[k // 8], (qb + 1) * (16 * NDMA))
                wait(pe, exp_ready, UNITS * qb + k - 1)
                for kh in range(KH):
                    bank = ps_s[:, k % 2, kh, :]
                    for g in range(G):
                        rhs = qbd[:, k // 8, g, :, :].rearrange("p h (j b q) -> p (h j) b q", j=J, b=8)[:, :, k % 8, :]
                        nc.tensor.matmul(bank[:, P * g:P * g + P], kst[:, g, S * k + P * kh:S * k + P * kh + P], rhs,
                                         start=(g == 0), stop=False, skip_group_check=True)
                    for q in range(Q0):
                        rhs = qrel[:, k // 8, :, :, :].rearrange("p h j (b q) -> p (h j) b q", b=8)[:, :, k % 8, q]
                        lhsT = e4[:, bass.ds(qb * -QN + (P * kh - q + ESTART), P)]
                        ins = nc.tensor.matmul(bank.rearrange("p (m q) -> p m q", q=Q0)[:, :, q], lhsT, rhs,
                                               start=False, stop=(q == Q0 - 1), skip_group_check=True)
                    ins.then_inc((half_ready, scores_ready)[kh], 1)

            def pv(qb, k):
                n = UNITS * qb + k
                pe.wait_ge(hi_ready, n + 1)
                pe.wait_ge(lo_ready, n + 1)
                pe.wait_ge(pool_lo_ready, n + 1)
                wait(pe, obd_ready, n)
                for g in range(G):
                    for kh in range(KH):
                        hi, lo = (probs[:, k // 8, x, kh, k % 8, P * g:P * g + P] for x in range(2))
                        val = v_sb[:, KH * k + kh, g, :]
                        nc.tensor.matmul(o_ps[:, g, :], hi, val[:, 0:VD + 1], start=(g == 0 and kh == 0), stop=False,
                                         skip_group_check=True)
                        nc.tensor.matmul(o_ps[:, g, 0:VD], hi, val[:, VD + 1:VC], start=False, stop=False,
                                         skip_group_check=True)
                        ins = nc.tensor.matmul(o_ps[:, g, :], lo, val[:, 0:VD + 1], start=False,
                                               stop=(g == G - 1 and kh == KH - 1), skip_group_check=True)
                ins.then_inc(pv_ready, 1)

            def transposed(qb, k):
                pe.wait_ge(obd_ready, UNITS * qb + k + 1)
                if k % 8 == 0:
                    wait(pe, oT_copied, BG * qb + k // 8)
                nc.tensor.matmul(y_ps[:, k % 8, :], obd[:, k % 2, :, :, :].rearrange("p g h d -> p (g h d)"), sel[:, :],
                                 start=True, stop=True).then_inc(oT_ready, 1)

            def relative(qb, bg, part):
                first, last = sum(REL_PARTS[:part]), sum(REL_PARTS[:part + 1])
                if first % QH == 0:
                    wait(pe, rel_copied, 2 * (BG * qb + bg) + first // QH)
                for q in range(first, last):
                    for kh in range(KH):
                        hi, lo = (probs[:, bg, x, kh, :, :].rearrange("p b (h q) -> p (b h) q", q=QN)[:, :, q] for x in range(2))
                        win = gv[:, bass.ds(qb * -QN + (P * kh - q + S - 1), 1), :][:, 0, :]
                        nc.tensor.matmul(r_ps[:, q % QH, :], hi, win, start=(q % QH == 0 and kh == 0), stop=False,
                                         skip_group_check=True)
                        ins = nc.tensor.matmul(r_ps[:, q % QH, 0:HD + 1], lo, win[:, 0:HD + 1], start=False,
                                               stop=(q % QH == QH - 1 and kh == KH - 1), skip_group_check=True)
                if last % QH == 0:
                    ins.then_inc(rel_ready, 1)

            def relative_step(qb, k):
                for bg in range(BG):
                    for back in range(2):
                        part = k + UNITS * back - (10 + 8 * bg)
                        if 0 <= part < len(REL_PARTS) and not (back and isinstance(qb, int) and qb == 0):
                            relative(qb - back, bg, part)

            def body(qb, last):
                for k in range(UNITS):
                    n = UNITS * qb + k
                    pe.wait_ge(max_ready, n + 1)
                    wait(pe, mcol_ready, n)
                    for g in range(G):
                        ins = nc.tensor.transpose(ps_tb[:, g, :], mx[:, k % 2, P * g:P * g + P], identb[:, :])
                    ins.then_inc(maxT_ready, 1)
                    if unit(qb, k - 2):
                        pv(*unit(qb, k - 2))
                    if k < UNITS - 1:
                        scores(qb, k + 1)
                    elif not last:
                        scores(qb + 1, 0)
                    relative_step(qb, k)
                    pe.wait_ge(mdiag_ready, n + 1)
                    for kh in range(KH):
                        ins = nc.tensor.matmul(ps_s[:, k % 2, kh, :], minus1[:, :], mdiag[:, :, :].rearrange("p g n -> p (g n)"),
                                               start=False, stop=True, skip_group_check=True)
                    ins.then_inc(shifted, 1)
                    if unit(qb, k - 2):
                        transposed(*unit(qb, k - 2))
            scores(0, 0)
            loop(pe, body)
            for k in (UNITS - 2, UNITS - 1):
                pv(NQB - 1, k)
                transposed(NQB - 1, k)
            relative(NQB - 1, 0, len(REL_PARTS) - 1)
            for part in range(len(REL_PARTS)):
                relative(NQB - 1, 1, part)

        @block.scalar
        def _(act):
            def copy_oT(qb, bg):
                act.wait_ge(oT_ready, 8 * (BG * qb + bg + 1))
                nc.scalar.activation(attT[:, 8 * bg:8 * bg + 8, bass.ds(qb * QN, QN)], y_ps[:, :, :],
                                     ACT.Copy).then_inc(oT_copied, 1)

            def copy_half(qb, k):
                n = UNITS * qb + k
                act.wait_ge(half_ready, n + 1)
                wait(act, max_ready, n - 1)
                nc.scalar.activation(s0[:, k % 2, :], ps_s[:, k % 2, 0, :], ACT.Copy).then_inc(half_copied, 1)

            def exponentials(qb, k):
                n = UNITS * qb + k
                act.wait_ge(shifted, n + 1)
                wait(act, lo_ready, n - 1)
                wait(act, pool_lo_ready, n - 1)
                nc.scalar.activation(p32[:, k % 2, :, :], ps_s[:, k % 2, :, :], ACT.Exp, scale=SCALE).then_inc(exp_ready, 1)

            def high_part(qb, k):
                n = UNITS * qb + k
                act.wait_ge(exp_ready, n + 1)
                if k % 8 == 0:
                    wait(act, rel_ready, 2 * (BG * qb + k // 8 - 1))
                nc.scalar.activation(probs[:, k // 8, 0, :, k % 8, :], p32[:, k % 2, :, :], ACT.Copy).then_inc(hi_ready, 1)

            def body(qb, last):
                for k in range(UNITS):
                    before = unit(qb, k - 1)
                    if before:
                        exponentials(*before)
                    if k < UNITS - 1:
                        copy_half(qb, k + 1)
                    elif not last:
                        copy_half(qb + 1, 0)
                    if before:
                        high_part(*before)
                    if k == 10:
                        copy_oT(qb, 0)
                    if k == 2 and unit(qb, -1):
                        copy_oT(qb - 1, 1)
            copy_half(0, 0)
            act.wait_ge(q_out[1], 32)
            loop(act, body)
            exponentials(NQB - 1, UNITS - 1)
            high_part(NQB - 1, UNITS - 1)
            copy_oT(NQB - 1, 1)

        def low_part(eng, engine, qb, k, kh, done):
            eng.wait_ge(hi_ready, UNITS * qb + k + 1)
            engine.tensor_tensor(probs[:, k // 8, 1, kh, k % 8, :], p32[:, k % 2, kh, :],
                                 probs[:, k // 8, 0, kh, k % 8, :], ALU.subtract).then_inc(done, 1)

        @block.gpsimd
        def _(pool):
            def body(qb, last):
                for k in range(UNITS):
                    low_part(pool, nc.gpsimd, qb, k, 1, pool_lo_ready)
            loop(pool, body)

        @block.vector
        def _(dve):
            def maximum(qb, k):
                n = UNITS * qb + k
                dve.wait_ge(half_copied, n + 1)
                dve.wait_ge(scores_ready, n + 1)
                nc.vector.tensor_tensor(mx[:, k % 2, :], s0[:, k % 2, :], ps_s[:, k % 2, 1, :], ALU.max).then_inc(max_ready, 1)

            def mask_outputs(qb, k):
                n = UNITS * qb + k
                dve.wait_ge(pv_ready, n + 1)
                nc.vector.reciprocal(rden[:, :], o_ps[:, :, VD]).then_inc(rden_ready, 1)
                dve.wait_ge(rden_ready, n + 1)
                nc.vector.tensor_tensor(rmask[:, :, :], rden[:, :].rearrange("p (g o) -> p g o", o=1).to_broadcast([P, G, HH]),
                                        hmask[:, :].rearrange("p (o h) -> p o h", o=1).to_broadcast([P, G, HH]),
                                        ALU.mult).then_inc(rmask_ready, 1)
                dve.wait_ge(rmask_ready, n + 1)
                wait(dve, oT_ready, n - 1)
                nc.vector.tensor_tensor(obd[:, k % 2, :, :, :], o_ps[:, :, 0:VD].rearrange("p g (h d) -> p g h d", h=HH),
                                        rmask[:, :, :].rearrange("p g (h o) -> p g h o", o=1).to_broadcast([P, G, HH, HD]),
                                        ALU.mult).then_inc(obd_ready, 1)

            def copy_relative(qb, bg, half):
                done = 2 * (BG * qb + bg) + half + 1
                dve.wait_ge(rel_ready, done)
                nc.vector.reciprocal(rrden[:, :], r_ps[:, :, HD]).then_inc(rrden_ready, 1)
                pairs = bass.AP(tensor=r_ps.tensor, offset=r_ps.offset,
                                ap=[list(r_ps.ap[0]), [RC, QH], [1, HD], [HD + 1, 2]])
                nc.vector.tensor_reduce(rsum[:, :, :], pairs, X_AXIS, ALU.add).then_inc(rsum_ready, 1)
                dve.wait_ge(rrden_ready, done)
                dve.wait_ge(rsum_ready, done)
                nc.vector.tensor_tensor(xr[:, bg, bass.ds(qb * QN + QH * half, QH), :], rsum[:, :, :],
                                        rrden[:, :].rearrange("p (q o) -> p q o", o=1).to_broadcast([P, QH, HD]),
                                        ALU.mult).then_inc(rel_copied, 1)

            def body(qb, last):
                for k in range(UNITS):
                    n = UNITS * qb + k
                    dve.wait_ge(maxT_ready, n + 1)
                    nc.vector.tensor_reduce(mcol[:, k % 2, :], ps_tb, X_AXIS, ALU.max).then_inc(mcol_ready, 1)
                    dve.wait_ge(mcol_ready, n + 1)
                    wait(dve, shifted, n)
                    nc.vector.tensor_tensor(mdiag[:, :, :], identb[:, :].rearrange("p (o n) -> p o n", o=1).to_broadcast([P, G, P]),
                                            mcol[:, k % 2, :].rearrange("p (g o) -> p g o", o=1).to_broadcast([P, G, P]),
                                            ALU.mult).then_inc(mdiag_ready, 1)
                    if unit(qb, k - 2):
                        mask_outputs(*unit(qb, k - 2))
                    if k < UNITS - 1:
                        maximum(qb, k + 1)
                    elif not last:
                        maximum(qb + 1, 0)
                    if unit(qb, k - 1):
                        low_part(dve, nc.vector, *unit(qb, k - 1), 0, lo_ready)
                    for bg in range(BG):
                        for half in range(2):
                            at = 12 + 8 * bg + 4 * half
                            if k == at % UNITS and (at < UNITS or unit(qb, -1)):
                                copy_relative(qb - at // UNITS, bg, half)
            maximum(0, 0)
            loop(dve, body)
            low_part(dve, nc.vector, NQB - 1, UNITS - 1, 0, lo_ready)
            for k in (UNITS - 2, UNITS - 1):
                mask_outputs(NQB - 1, k)
            copy_relative(NQB - 1, 0, 1)
            for half in range(2):
                copy_relative(NQB - 1, 1, half)


def build_last(nc, v):
    xr, attT, identf, wo_sb, big, y_dram, out = v["xr"], v["attT"], v["identf"], v["wo_sb"], v["big"], v["y_dram"], v["out"]
    ps_s, ps_t, ps_o, ps_r, ps_y = v["ps_s"], v["ps_t"], v["ps_o"], v["ps_r"], v["ps_y"]
    NT = TOK // P
    at = NT * D
    y_sb = big[:, 0:at].rearrange("p (t n) -> p t n", n=D)
    orel = big[:, at:at + 2 * 8 * D].rearrange("p (s b h d) -> p s b h d", s=2, b=8, h=H)
    at += 2 * 8 * D
    oT = big[:, at:at + 2 * 8 * P].rearrange("p (s n) -> p s n", s=2)

    ctx = ExitStack()
    with ctx:
        def sem(name):
            return ctx.enter_context(nc.semaphore(name))

        y_in, d_ready, orel_ready = sem("y_in"), sem("d_ready"), sem("orel_ready")
        relT_ready, oT_ready, out_ready, y_ready, y_out = sem("relT_ready"), sem("oT_sum_ready"), sem("out_ready"), sem("y_sum_ready"), sem("y_sum_out")
        block = ctx.enter_context(nc.Block())
        PARTS_ = [(bg, qh) for bg in range(BG) for qh in range(KH)]
        out_t = out.rearrange("b (h p) d -> h p b d", p=P)
        y_v = y_sb.rearrange("p (b h) d -> p h b d", h=KH)

        @block.sync
        def _(sp):
            sp.dma_start(y_sb, y_dram[:, :, :]).then_inc(y_in, 16)
            for m, (bg, qh) in enumerate(PARTS_):
                sp.wait_ge(y_ready, 2 * (m + 1))
                sp.dma_start(out_t[qh, :, 8 * bg:8 * bg + 8, :], y_v[:, qh, 8 * bg:8 * bg + 8, :]).then_inc(y_out, 16)
            sp.wait_ge(y_out, 16 * len(PARTS_))

        @block.tensor
        def _(pe):
            for m, (bg, qh) in enumerate(PARTS_):
                for half in range(2):
                    wait(pe, orel_ready, 2 * (m - 1) + half + 1)
                    for d in range(4):
                        ins = nc.tensor.transpose(ps_s[:, 0, half, P * d:P * d + P],
                                                  xr[:, bg, P * qh:P * qh + P, 4 * half + d], identf[:, :])
                    ins.then_inc(d_ready, 1)
                pe.wait_ge(orel_ready, 2 * (m + 1))
                for half in range(2):
                    wait(pe, oT_ready, 2 * (m - 1) + half + 1)
                    for b in range(4):
                        ins = nc.tensor.transpose(ps_s[:, 1, half, P * b:P * b + P],
                                                  orel[:, m % 2, 4 * half + b, :, :].rearrange("p h d -> p (h d)"), identf[:, :])
                    ins.then_inc(relT_ready, 1)
                for half in range(2):
                    pe.wait_ge(oT_ready, 2 * m + half + 1)
                    wait(pe, y_ready, 2 * (m - 1) + half + 1)
                    for b in range(4):
                        ins = nc.tensor.matmul((ps_t, ps_o)[half][:, P * b:P * b + P],
                                               oT[:, m % 2, P * (4 * half + b):P * (4 * half + b) + P], wo_sb[:, :],
                                               start=True, stop=True)
                    ins.then_inc(out_ready, 1)

        @block.scalar
        def _(act):
            for m in range(len(PARTS_)):
                for half in range(2):
                    act.wait_ge(d_ready, 2 * m + half + 1)
                    wait(act, relT_ready, 2 * (m - 1))
                    nc.scalar.activation(orel[:, m % 2, :, :, 4 * half:4 * half + 4],
                                         ps_s[:, 0, half, :].rearrange("p (d b h) -> p b h d", d=4, b=8),
                                         ACT.Copy).then_inc(orel_ready, 1)

        @block.vector
        def _(dve):
            dve.wait_ge(y_in, 16)
            for m, (bg, qh) in enumerate(PARTS_):
                for half in range(2):
                    dve.wait_ge(relT_ready, 2 * m + half + 1)
                    b0 = 8 * bg + 4 * half
                    nc.vector.tensor_tensor(oT[:, m % 2, 4 * P * half:4 * P * half + 4 * P].rearrange("p (b q) -> p b q", b=4),
                                            ps_s[:, 1, half, :].rearrange("p (b q) -> p b q", b=4),
                                            attT[:, b0:b0 + 4, P * qh:P * qh + P], ALU.add).then_inc(oT_ready, 1)
                for half in range(2):
                    dve.wait_ge(out_ready, 2 * m + half + 1)
                    b0 = 8 * bg + 4 * half
                    nc.vector.tensor_tensor(y_v[:, qh, b0:b0 + 4, :], (ps_t, ps_o)[half][:, :].rearrange("p (b n) -> p b n", b=4),
                                            y_v[:, qh, b0:b0 + 4, :], ALU.add).then_inc(y_ready, 1)


def kernel(**inputs):
    import concourse.bacc as bacc
    from concourse.bass_utils import run_bass_kernel_spmd

    names = {"L0_attn_x": "x", "L0_attn_Wq": "wqT", "L0_attn_bq": "bq", "L0_attn_Wk": "wkT", "L0_attn_bk": "bk",
             "L0_attn_Wv": "wvT", "L0_attn_bv": "bv", "L0_attn_Wo": "woT", "L0_attn_bo": "bo",
             "L0_attn_rel_k": "rel_kT", "L0_attn_rel_v": "rel_v", "L0_ffn_W1": "w1T", "L0_ffn_b1": "b1",
             "L0_ffn_W2": "w2T", "L0_ffn_b2": "b2"}
    nc = bacc.Bacc("TRN2", target_bir_lowering=False, num_devices=1)
    arrays, args = {}, {}
    for name, short in names.items():
        a = np.asarray(inputs[name])
        a = np.ascontiguousarray(a.T if short.endswith("T") else a)
        arrays[f"in_{short}"] = a
        args[short] = nc.dram_tensor(f"in_{short}", a.shape, mybir.dt.from_np(a.dtype), kind="ExternalInput").ap()
    out = nc.dram_tensor("out", (B, S, D), F32, kind="ExternalOutput").ap()
    layer_kernel(nc, out=out, **args)
    r = run_bass_kernel_spmd(nc, [arrays], core_ids=[0])
    return r.results[0]["out"]
```

```python
import math
from contextlib import ExitStack

import numpy as np
import concourse.bass as bass
from concourse import mybir

F32 = mybir.dt.float32
F16 = mybir.dt.float16
BF16 = mybir.dt.bfloat16
ALU = mybir.AluOpType
ACT = mybir.ActivationFunctionType
X_AXIS = mybir.AxisListType.X

B, S, D = 16, 256, 128
H = 16
HD = D // H
M = 128
NREL = 2 * M + 1
FF = 4 * D
P = 128
TOK = B * S
KH = S // P
FT = FF // P
G, HH = 4, 4
PARTS = 3
KR = PARTS * 32
QN = 32
NQB = S // QN
J, Q0 = 4, 8
BG = B // 8
UNITS = B
COLS = H * QN
CH = 4
NCH = TOK // (CH * P)
VD = HH * HD
VC = 2 * VD + 1
RC = 2 * HD + 1
QH = QN // 2
LO = COLS // 2
REL_PARTS = (4, 4, 4, 4, 5, 5, 6)
EW = 2 * S - 1 - 24
ESTART = EW - S
EWIN = S + Q0 - 1
PAD = S - 1 - M
NU = 2 * S - P
LN_EPS = 1e-5
Q_EPS = 1e-5
SCALE = 1.0 / math.sqrt(HD)


def wait(eng, sem, value):
    if isinstance(value, int) and value <= 0:
        return
    eng.wait_ge(sem, value)


def layer_kernel(nc, x, wqT, bq, wkT, bk, wvT, bv, woT, bo, rel_kT, rel_v, w1T, b1, w2T, b2, out):
    ctx = ExitStack()
    with ctx:
        def sb(name, shape, dt):
            return ctx.enter_context(nc.sbuf_tensor(name, shape, dt))

        def sem(name):
            return ctx.enter_context(nc.semaphore(name))

        q_dram = nc.dram_tensor("q_dram", (2, D, TOK), F16, kind="Internal").ap()
        relv_dram = nc.dram_tensor("relv_dram", (2 * S, HD), F32, kind="Internal").ap()
        y_dram = nc.dram_tensor("y_dram", (P, TOK // P, D), F32, kind="Internal").ap()

        identf = sb("identf", [P, P], F32)
        identb = sb("identb", [P, P], BF16)
        minus1 = sb("minus1", [P, P], BF16)
        sel = sb("sel", [P, QN], F16)
        hmask = sb("hmask", [P, HH], F32)
        kst = sb("kst", [KR, G, TOK], F16)
        e4 = sb("e4", [KR, EW], F16)
        qbd = sb("qbd", [KR, 2, G, HH, J * 8 * Q0], F16)
        qrel = sb("qrel", [KR, 2, H, J, 8 * Q0], F16)
        v_sb = sb("v_sb", [P, TOK // P, G, VC], F16)
        gv = sb("gv", [P, NU, RC], F16)
        ewin = sb("ewin", [KR, EWIN], F16)
        gwin = sb("gwin", [P, KH, QN, RC], F16)
        attT = sb("attT", [P, B, S], F32)
        xr = sb("xr", [P, BG, S, HD], F32)
        big = sb("big", [P, 2 * 8 * KH * COLS], F32)
        probs = big[:, :].bitcast(F16).rearrange("p (s x k b c) -> p s x k b c", s=2, x=2, b=8, k=KH)
        at = [0]

        def carve(shape, dt=F32):
            n = int(np.prod(shape)) * (2 if dt == F16 else 4) // 4
            v = big[:, at[0]:at[0] + n]
            at[0] += n
            assert at[0] <= 2 * 8 * KH * COLS
            if dt == F16:
                v = v.bitcast(F16)
            if len(shape) == 1:
                return v
            names = " ".join("abcd"[:len(shape)])
            return v.rearrange(f"p ({names}) -> p {names}", **{c: n for c, n in zip("abcd", shape)})

        x_sb = carve([TOK // P, D])
        xn = carve([2, CH, D])
        xT = carve([2, CH * P])
        hid = carve([2, FT, CH * P], F16)
        q_hi, q_lo = carve([TOK], F16), carve([TOK], F16)
        k_hi, k_lo = carve([TOK], F16), carve([TOK], F16)
        p32 = sb("p32", [P, 2, KH, COLS], F32)
        p32_flat = p32[:, :, :, :].rearrange("p s k c -> p (s k c)")
        w1_sb = p32_flat[:, 0:2 * FF].rearrange("p (w n) -> p w n", w=2)
        eraw = p32_flat[0:KR, 2 * FF:2 * FF + EW]
        gvraw = attT[:, :, :].rearrange("p b s -> p (b s)")[:, 0:NU * HD].rearrange("p (u d) -> p u d", d=HD)
        xr_flat = xr[:, :, :, :].rearrange("p b s d -> p (b s d)")
        place = [0]

        def in_xr(n, dt=F32):
            words = n * (2 if dt == F16 else 4) // 4
            piece = xr_flat[:, place[0]:place[0] + words]
            place[0] += words
            return piece.bitcast(F16) if dt == F16 else piece

        wqkv = in_xr(3 * D).rearrange("p (w n) -> p w n", w=3)
        bvb, bobb, bo2b, onesf = in_xr(D), in_xr(D), in_xr(D), in_xr(P)
        w16 = in_xr(2 * FF, F16).rearrange("p (w n) -> p w n", w=2)
        hf = in_xr(2 * CH * P).rearrange("p (s n) -> p s n", s=2)
        xT16 = in_xr(4 * CH * P, F16).rearrange("p (s x n) -> p s x n", s=2, x=2)
        bhl = in_xr(2 * D, F16).rearrange("p (w n) -> p w n", w=2)
        pick = in_xr(P, F16)
        bcol = sb("bcol", [P, 2 + FT], F32)
        rcol = sb("rcol", [KR, 2], F32)
        wabs = sb("wabs", [P, 2], F32)
        wdiv = sb("wdiv", [P, 2], F32)
        wthr = sb("wthr", [P, 4], F32)
        wneg = attT[:, :, :].rearrange("p b s -> p (b s)")[:, NU * HD:NU * HD + 2 * FF].rearrange("p (w n) -> p w n", w=2)
        vare = sb("vare", [P, 2, CH], F32)
        rstd = sb("rstd", [P, 2, CH], F32)
        neghalf = sb("neghalf", [P, CH], F32)
        s0 = sb("s0", [P, COLS], BF16)
        mx = sb("mx", [P, COLS], BF16)
        mcol = sb("mcol", [P, 2, G], F32)
        mdiag = sb("mdiag", [P, G, P], BF16)
        rden = sb("rden", [P, G], F32)
        rmask = sb("rmask", [P, G, HH], F32)
        obd = sb("obd", [P, 2, G, HH, HD], F32)
        obd_flat = obd[:, :, :, :, :].rearrange("p s g h d -> p (s g h d)")
        stats = obd_flat[:, 0:2 * CH * 6].rearrange("p (s t n) -> p s t n", s=2, t=CH)
        mv = obd_flat[:, 2 * CH * 6:2 * CH * 9].rearrange("p (s t n) -> p s t n", s=2, t=CH)
        obd2 = sb("obd2", [P, 2, 2, G, HH, HD], F16)
        rrden = sb("rrden", [P, QH], F32)
        rsum = sb("rsum", [P, QH, HD], F32)

        ps_s = ctx.enter_context(nc.psum_tensor("ps_s", [P, 2, KH, COLS], F32))
        ps_t = ctx.enter_context(nc.psum_tensor("ps_t", [P, 512], F32))
        ps_o = ctx.enter_context(nc.psum_tensor("ps_o", [P, 512], F32))
        ps_r = ctx.enter_context(nc.psum_tensor("ps_r", [P, 512], F32))
        ps_y = ctx.enter_context(nc.psum_tensor("ps_y", [P, 512], F32))

        q_out = [sem(f"q_out{i}") for i in range(BG)]
        q_in = [sem(f"q_in{i}") for i in range(BG)]
        kst_in, kst_last, y_out = sem("kst_in"), sem("kst_last"), sem("y_out")

        build_first(nc, locals())
        build_main(nc, locals())


def load_queries(eng, v, qb, bg):
    for s in range(PARTS):
        src = v["q_dram"].rearrange("s (h d) (a n c) -> s a h d n c", d=HD, a=BG, n=NQB)[1 if s == 2 else 0, bg]
        for k in range(4):
            rows = slice(32 * s + HD * k, 32 * s + HD * k + HD)
            own = src.rearrange("(g k) d n c -> k d g n c", k=HH)[k, :, :, bass.ds(qb, 1), :][:, :, 0, :]
            eng.dma_start(v["qbd"][rows, bg, :, k, :], own).then_inc(v["q_in"][bg], 16)
            own = src.rearrange("h d n c -> d h n c")[:, :, bass.ds(qb, 1), 64 * k:64 * k + 64][:, :, 0, :]
            eng.dma_start(v["qrel"][rows, bg, :, k, :], own).then_inc(v["q_in"][bg], 16)


def stack_keys(eng, v, i, signal):
    cols = bass.ds(i * (2 * CH * P), 2 * CH * P)
    for g in range(G):
        for s, part in enumerate(("k_hi", "k_lo", "k_hi")):
            eng.dma_start(v["kst"][32 * s:32 * s + 32, g, cols], v[part][32 * g:32 * g + 32, cols]).then_inc(signal, 16)


def save_rest(eng, v, i):
    own = bass.ds(i * (2 * CH), 2 * CH)
    eng.dma_start(v["y_dram"][:, own, :], v["x_sb"][:, own, :]).then_inc(v["y_out"], 16)


def build_first(nc, v):
    x, out = v["x"], v["out"]
    q_dram, relv_dram, y_dram = v["q_dram"], v["relv_dram"], v["y_dram"]
    w16, hf, xT16, bhl, pick = v["w16"], v["hf"], v["xT16"], v["bhl"], v["pick"]
    x_sb, xn, xT, hid = v["x_sb"], v["xn"], v["xT"], v["hid"]
    q_hi, q_lo, k_hi, k_lo = v["q_hi"], v["q_lo"], v["k_hi"], v["k_lo"]
    kst, e4, v_sb, gv, gvraw, eraw = v["kst"], v["e4"], v["v_sb"], v["gv"], v["gvraw"], v["eraw"]
    wqkv, bvb, bobb, bo2b, onesf, bcol = v["wqkv"], v["bvb"], v["bobb"], v["bo2b"], v["onesf"], v["bcol"]
    wthr, wneg = v["wthr"], v["wneg"]
    w1_sb, wabs, wdiv, rcol = v["w1_sb"], v["wabs"], v["wdiv"], v["rcol"]
    stats, mv, vare, rstd, neghalf = v["stats"], v["mv"], v["vare"], v["rstd"], v["neghalf"]
    identf, identb, minus1, sel, hmask = v["identf"], v["identb"], v["minus1"], v["sel"], v["hmask"]
    ps_s, ps_t, ps_o, ps_r, ps_y = v["ps_s"], v["ps_t"], v["ps_o"], v["ps_r"], v["ps_y"]
    ps_f = ps_s[:, 1, 1, :]

    ctx = ExitStack()
    with ctx:
        def sem(name):
            return ctx.enter_context(nc.semaphore(name))

        w_in, ff_in, pad_in = sem("w_in"), sem("ff_in"), sem("pad_in")
        x_in = [sem(f"x_in{i}") for i in range(4)]
        relv_out, gv_in, pads_ready, e_in = sem("relv_out"), sem("gv_in"), sem("pads_ready"), sem("e_in")
        ones_ready, ident_ready, zero_ready = sem("ones_ready"), sem("ident_ready"), sem("zero_ready")
        dve_step, tab_ready, zero_q = sem("dve_step"), sem("tab_ready"), sem("zero_q")
        wabs_ready, gamma_ready, wq_ready = sem("wabs_ready"), sem("gamma_ready"), sem("wq_ready")
        var_ready, rstd_ready, xn_ready = sem("var_ready"), sem("rstd_ready"), sem("xn_ready")
        xnT_ready, xT_ready = sem("xnT_ready"), sem("xT_ready")
        q_ready, k_ready, v_ready = sem("q_ready"), sem("k_ready"), sem("v_ready")
        qhi_ready, khi_ready, qlo_ready, klo_ready = sem("qhi_ready"), sem("khi_ready"), sem("qlo_ready"), sem("klo_ready")
        v_copied, h_ready, hid_used, f_ready, y_ready = sem("v_copied"), sem("h_ready"), sem("hid_used"), sem("f_ready"), sem("y_ready")
        hhi_ready, hlo_ready, xhi_ready, xlo_ready = sem("hhi_ready"), sem("hlo_ready"), sem("xhi_ready"), sem("xlo_ready")
        bias_ready = sem("bias_ready")
        q_out, kst_in, y_out = v["q_out"], v["kst_in"], v["y_out"]
        block = ctx.enter_context(nc.Block())

        x_t = x.rearrange("b (h p) d -> p (b h) d", p=P)

        def loop(eng, body):
            body(0, False)
            with eng.Fori(1, NCH // 2 - 1) as i:
                body(i, False)
            body(NCH // 2 - 1, True)

        def tiles(i, p, n=CH):
            return bass.ds(i * (2 * n) + p * n, n)

        def save_queries(eng, bg):
            eng.wait_ge(qlo_ready, NCH // 2 * (bg + 1))
            for s, src in enumerate((q_hi, q_lo)):
                eng.dma_start(q_dram[s].rearrange("p (a m c) -> a p m c", a=BG, m=NQB * J)[bg],
                              src.rearrange("p (m a c) -> p m a c", a=BG, m=NQB * J)[:, :, bg, :]).then_inc(q_out[bg], 16)

        @block.sync
        def _(sp):
            half = TOK // P // 2
            sp.dma_start(x_sb[:, 0:CH, :], x_t[:, 0:CH, :]).then_inc(x_in[0], 16)
            sp.dma_start(x_sb[:, CH:2 * CH, :], x_t[:, CH:2 * CH, :]).then_inc(x_in[1], 16)
            sp.dma_start(wqkv[:, 0, :], v["wqT"]).then_inc(w_in, 16)
            sp.dma_start(wqkv[:, 1, :], v["wkT"]).then_inc(w_in, 16)
            sp.dma_start(wqkv[:, 2, :], v["wvT"]).then_inc(w_in, 16)
            sp.dma_start(bcol[:, 0:1], v["bq"].rearrange("(p o) -> p o", o=1)).then_inc(w_in, 16)
            sp.dma_start(bcol[:, 1:2], v["bk"].rearrange("(p o) -> p o", o=1)).then_inc(w_in, 16)
            with nc.allow_non_contiguous_dma(reason="512 bias values"):
                sp.dma_start(bcol[:, 2:2 + FT], v["b1"].rearrange("(t p) -> p t", p=P)).then_inc(w_in, 16)
            for t, src in ((bvb, "bv"), (bobb, "bo"), (bo2b, "b2")):
                sp.dma_start(t, v[src].rearrange("(o d) -> o d", o=1).to_broadcast([P, D])).then_inc(w_in, 16)
            sp.dma_start(x_sb[:, 2 * CH:half, :], x_t[:, 2 * CH:half, :]).then_inc(x_in[2], 16)
            sp.dma_start(x_sb[:, half:, :], x_t[:, half:, :]).then_inc(x_in[3], 16)
            sp.dma_start(relv_dram[0:PAD, :], v["rel_v"][0:1, :].to_broadcast([PAD, HD])).then_inc(relv_out, 16)
            sp.dma_start(relv_dram[PAD:PAD + NREL, :], v["rel_v"][:, :]).then_inc(relv_out, 16)
            sp.dma_start(relv_dram[PAD + NREL:2 * S, :],
                         v["rel_v"][NREL - 1:NREL, :].to_broadcast([2 * S - PAD - NREL, HD])).then_inc(relv_out, 16)
            sp.wait_ge(relv_out, 48)
            win = bass.AP(tensor=relv_dram.tensor, offset=0, ap=[[HD, P], [1, NU * HD]])
            sp.dma_start(gvraw.rearrange("p u d -> p (u d)"), win).then_inc(gv_in, 16)
            sp.wait_ge(pads_ready, 2)
            for s in range(PARTS):
                for j in range(J):
                    r0, c0 = 32 * s + HD * j, PAD - 24 + 8 * j
                    sp.dma_start(eraw[r0:r0 + HD, c0:c0 + NREL], v["rel_kT"]).then_inc(e_in, 16)

            for half, (i0, i1) in enumerate(((0, NCH // 4), (NCH // 4, NCH // 2 - 1))):
                with sp.Fori(i0, i1) as i:
                    sp.wait_ge(klo_ready, 2 * i + 2)
                    stack_keys(sp, v, i, kst_in)
                    sp.wait_ge(y_ready, 2 * i + 2)
                    save_rest(sp, v, i)
                if half == 0:
                    save_queries(sp, 0)
            sp.wait_ge(q_out[0], 32)
            sp.wait_ge(zero_q, 2)
            load_queries(sp, v, 0, 0)
            save_queries(sp, 1)

        @block.scalar
        def _(act):
            act.dma_start(w1_sb[:, 0, :], v["w1T"]).then_inc(ff_in, 16)
            act.dma_start(w1_sb[:, 1, :].rearrange("p (t n) -> p t n", t=FT),
                          v["w2T"].rearrange("(t p) n -> p t n", p=P)).then_inc(ff_in, 16)
            with nc.allow_non_contiguous_dma(reason="end rows of rel_k"):
                for end in range(2):
                    src = bass.AP(tensor=v["rel_kT"].tensor, offset=end * (NREL - 1), ap=[[0, KR // HD], [NREL, HD], [1, 1]])
                    act.dma_start(rcol[:, end:end + 1], src).then_inc(pad_in, 16)

            def copy_xT(c, p):
                act.wait_ge(xnT_ready, c + 1)
                wait(act, v_ready, c - 1)
                nc.scalar.activation(xT[:, p, :], ps_t[:, :], ACT.Copy).then_inc(xT_ready, 1)
                nc.scalar.activation(xT16[:, p, 0, :], ps_t[:, :], ACT.Copy).then_inc(xhi_ready, 1)

            def hidden(c, f):
                act.wait_ge(h_ready, c * FT + f + 1)
                wait(act, hlo_ready, c * FT + f - 1)
                nc.scalar.activation(hf[:, f % 2, :], ps_s[:, 0, f % 2, :], ACT.Relu, bias=bcol[:, 2 + f:3 + f])
                wait(act, hid_used, (c - 1) * FT + f + 1)
                nc.scalar.activation(hid[:, 0, f, :], ps_s[:, 0, f % 2, :], ACT.Relu,
                                     bias=bcol[:, 2 + f:3 + f]).then_inc(hhi_ready, 1)

            copy_xT(0, 0)
            act.wait_ge(w_in, 144)

            def body(i, last):
                for p in range(2):
                    c = 2 * i + p
                    act.wait_ge(q_ready, c + 1)
                    for b in range(2):
                        dst = q_hi.rearrange("p (m b q) -> p m b q", m=NQB * J, b=B)[:, :, bass.ds(4 * i + 2 * p + b, 1), :]
                        ins = nc.scalar.activation(dst[:, :, 0, :], ps_o[:, S * b:S * b + S].rearrange("p (m q) -> p m q", q=Q0),
                                                   ACT.Identity, bias=bcol[:, 0:1])
                    ins.then_inc(qhi_ready, 1)
                    if not (last and p == 1):
                        copy_xT(c + 1, 1 - p)
                    hidden(c, 0)
                    hidden(c, 1)
                    act.wait_ge(k_ready, c + 1)
                    nc.scalar.activation(k_hi[:, tiles(i, p, CH * P)], ps_r[:, :], ACT.Identity,
                                         bias=bcol[:, 1:2]).then_inc(khi_ready, 1)
                    hidden(c, 2)
                    hidden(c, 3)
            loop(act, body)

        @block.gpsimd
        def _(pool):
            nc.gpsimd.memset(identf[:, :], 0.0).then_inc(zero_ready, 1)
            nc.gpsimd.memset(onesf, 1.0).then_inc(ones_ready, 1)
            nc.gpsimd.memset(neghalf[:, :], -0.5).then_inc(ones_ready, 1)
            pool.wait_ge(zero_ready, 1)
            nc.gpsimd.affine_select(out=identf[:, :], in_=identf[:, :], compare_op=ALU.not_equal, fill=1.0, base=0,
                                    pattern=[[-1, P]], channel_multiplier=1).then_inc(ident_ready, 1)
            pool.wait_ge(ones_ready, 2)

            def inverse_deviation(c, p):
                pool.wait_ge(var_ready, c + 1)
                nc.gpsimd.tensor_tensor(rstd[:, p, :], vare[:, p, :], neghalf[:, :], ALU.pow).then_inc(rstd_ready, 1)

            def hidden_low(c, f):
                pool.wait_ge(hhi_ready, c * FT + f + 1)
                nc.gpsimd.tensor_tensor(hid[:, 1, f, :], hf[:, f % 2, :], hid[:, 0, f, :], ALU.subtract).then_inc(hlo_ready, 1)

            inverse_deviation(0, 0)
            inverse_deviation(1, 1)
            nc.gpsimd.memset(v["qbd"][:, :, :, :, :].rearrange("p s g h c -> p (s g h c)").bitcast(F32), 0.0).then_inc(zero_q, 1)

            def body(i, last):
                for p in range(2):
                    if not last:
                        inverse_deviation(2 * i + p + 2, p)
                    for f in range(FT):
                        hidden_low(2 * i + p, f)
                    if isinstance(i, int) and i + p == 0:
                        nc.gpsimd.memset(v["qrel"][:, :, :, :, :].rearrange("p s h j c -> p (s h j c)").bitcast(F32), 0.0).then_inc(zero_q, 1)
            loop(pool, body)

        @block.vector
        def _(dve):
            done = [0]

            def step(ins):
                done[0] = done[0] + 1
                ins.then_inc(dve_step, 1)
                dve.wait_ge(dve_step, done[0])

            def statistics(i, p, c):
                for t in range(CH):
                    last = nc.vector.bn_stats(stats[:, p, t, :], x_sb[:, bass.ds(i * 2 * CH + p * CH + t, 1), :][:, 0, :])
                step(last)
                st, m = stats[:, p, :, :], mv[:, p, :, :]
                nc.vector.tensor_tensor(m[:, :, 0], st[:, :, 1], st[:, :, 4], ALU.add)
                nc.vector.tensor_tensor(m[:, :, 1], st[:, :, 1], st[:, :, 4], ALU.subtract)
                step(nc.vector.tensor_tensor(m[:, :, 2], st[:, :, 2], st[:, :, 5], ALU.add))
                nc.vector.tensor_scalar(m[:, :, 0], m[:, :, 0], 0.5, None, ALU.mult)
                nc.vector.tensor_scalar(m[:, :, 2], m[:, :, 2], 1.0 / D, LN_EPS, ALU.mult, ALU.add)
                step(nc.vector.tensor_tensor(m[:, :, 1], m[:, :, 1], m[:, :, 1], ALU.mult))
                nc.vector.scalar_tensor_tensor(out=vare[:, p, :], in0=m[:, :, 1], scalar=0.25, in1=m[:, :, 2],
                                               op0=ALU.mult, op1=ALU.add).then_inc(var_ready, 1)

            def normalize(i, p, c):
                dve.wait_ge(rstd_ready, c + 1)
                wait(dve, xnT_ready, c - 1)
                for t in range(CH):
                    last = nc.vector.tensor_scalar(xn[:, p, t, :], x_sb[:, bass.ds(i * 2 * CH + p * CH + t, 1), :][:, 0, :],
                                                   mv[:, p, t, 0:1], rstd[:, p, t:t + 1], ALU.subtract, ALU.mult)
                last.then_inc(xn_ready, 1)

            dve.wait_ge(x_in[0], 16)
            statistics(0, 0, 0)
            dve.wait_ge(x_in[1], 16)
            statistics(0, 1, 1)
            normalize(0, 0, 0)
            normalize(0, 1, 1)
            dve.wait_ge(w_in, 144)
            step(nc.vector.tensor_tensor(bo2b, bo2b, bobb, ALU.add))
            dve.wait_ge(ff_in, 32)
            for w in range(2):
                last = nc.vector.tensor_reduce(wabs[:, w:w + 1], w1_sb[:, w, :], X_AXIS, ALU.add,
                                               apply_absolute_value=True)
            last.then_inc(wabs_ready, 1)
            dve.wait_ge(gamma_ready, 1)
            step(nc.vector.tensor_scalar(wdiv[:, :], ps_f[:, 0:2], 1.0 / (FF * D), Q_EPS, ALU.mult, ALU.add))
            step(nc.vector.tensor_scalar(wthr[:, 0:2], wdiv[:, :], 0.5, None, ALU.mult))
            step(nc.vector.tensor_scalar(wthr[:, 2:4], wdiv[:, :], -0.5, None, ALU.mult))
            for w in range(2):
                step(nc.vector.tensor_scalar(wneg[:, w, :], w1_sb[:, w, :], wthr[:, 2 + w:3 + w], None, ALU.is_lt))
            for w in range(2):
                ins = nc.vector.scalar_tensor_tensor(out=w16[:, w, :], in0=w1_sb[:, w, :], scalar=wthr[:, w:w + 1],
                                                     in1=wneg[:, w, :], op0=ALU.is_gt, op1=ALU.subtract)
            ins.then_inc(wq_ready, 1)
            nc.vector.memset(pick[0:64, :], 0.0)
            nc.vector.tensor_copy(bhl[0:64, 0, :], bo2b[0:64, :])
            step(nc.vector.tensor_copy(bhl[0:64, 1, :], bvb[0:64, :]))
            for row in (0, 32):
                nc.vector.memset(pick[row:row + 1, :], 1.0)
            nc.vector.tensor_tensor(bhl[32:64, 0, :], bo2b[32:64, :], bhl[32:64, 0, :], ALU.subtract)
            nc.vector.tensor_tensor(bhl[32:64, 1, :], bvb[32:64, :], bhl[32:64, 1, :], ALU.subtract).then_inc(bias_ready, 1)
            dve.wait_ge(xhi_ready, 1)
            nc.vector.tensor_tensor(xT16[:, 0, 1, :], ps_t[:, :], xT16[:, 0, 0, :], ALU.subtract).then_inc(xlo_ready, 1)
            dve.wait_ge(pad_in, 32)
            mid = PAD + M
            nc.vector.tensor_copy(eraw[:, 0:mid], rcol[:, 0:1].to_broadcast([KR, mid])).then_inc(pads_ready, 1)
            nc.vector.tensor_copy(eraw[:, mid:], rcol[:, 1:2].to_broadcast([KR, EW - mid])).then_inc(pads_ready, 1)
            start = done[0]

            def body(i, last):
                done[0] = start + i * 6
                for p in range(2):
                    c = 2 * i + p
                    dve.wait_ge(qhi_ready, c + 1)
                    for b in range(2):
                        lo, hi = (t.rearrange("p (m b q) -> p m b q", m=NQB * J, b=B)[:, :, bass.ds(4 * i + 2 * p + b, 1), :][:, :, 0, :]
                                  for t in (q_lo, q_hi))
                        ins = nc.vector.scalar_tensor_tensor(
                            out=lo, in0=ps_o[:, S * b:S * b + S].rearrange("p (m q) -> p m q", q=Q0),
                            scalar=bcol[:, 0:1], in1=hi, op0=ALU.add, op1=ALU.subtract)
                    ins.then_inc(qlo_ready, 1)
                    if not last:
                        statistics(i + 1, p, c + 2)
                    if not (last and p == 1):
                        dve.wait_ge(xhi_ready, c + 2)
                        nc.vector.tensor_tensor(xT16[:, 1 - p, 1, :], ps_t[:, :], xT16[:, 1 - p, 0, :],
                                                ALU.subtract).then_inc(xlo_ready, 1)
                    if not (isinstance(i, int) and c == 0):
                        add_hidden(c - 1, bass.ds(i * (2 * CH) + (p * CH - CH), CH))
                    dve.wait_ge(khi_ready, c + 1)
                    nc.vector.scalar_tensor_tensor(
                        out=k_lo[:, tiles(i, p, CH * P)], in0=ps_r[:, :], scalar=bcol[:, 1:2],
                        in1=k_hi[:, tiles(i, p, CH * P)], op0=ALU.add, op1=ALU.subtract).then_inc(klo_ready, 1)
                    if not last:
                        normalize(i + 1, p, c + 2)
                    dve.wait_ge(v_ready, c + 1)
                    v4 = ps_y[:, :].rearrange("p (t g e) -> p t g e", t=CH, g=G)
                    v_hi = v_sb[:, tiles(i, p), :, 0:VD]
                    nc.vector.tensor_copy(v_hi, v4).then_inc(v_copied, 1)
                    dve.wait_ge(v_copied, 2 * c + 1)
                    nc.vector.tensor_tensor(v_sb[:, tiles(i, p), :, VD + 1:VC], v4, v_hi,
                                            ALU.subtract).then_inc(v_copied, 1)
                    if isinstance(i, int) and i == 0 and p == 1:
                        dve.wait_ge(e_in, 16 * PARTS * J)
                        nc.vector.tensor_copy(e4[:, :], eraw[:, :]).then_inc(tab_ready, 1)
                        dve.wait_ge(tab_ready, 1)
                        nc.vector.tensor_tensor(e4[32:64, :], eraw[32:64, :], e4[32:64, :], ALU.subtract)
                        rel_v_table(0)
                    if last:
                        rel_v_table(1 + p)

            def add_hidden(c, own):
                dve.wait_ge(f_ready, c + 1)
                nc.vector.tensor_tensor(x_sb[:, own, :], ps_f.rearrange("p (t n) -> p t n", t=CH),
                                        x_sb[:, own, :], ALU.add).then_inc(y_ready, 1)
            def rel_v_table(third):
                dve.wait_ge(gv_in, 16)
                own = slice(NU // 3 * third, NU // 3 * third + NU // 3)
                nc.vector.tensor_copy(gv[:, own, 0:HD], gvraw[:, own, :]).then_inc(tab_ready, 1)
                dve.wait_ge(tab_ready, 2 + third)
                nc.vector.tensor_tensor(gv[:, own, HD + 1:RC], gvraw[:, own, :], gv[:, own, 0:HD], ALU.subtract)

            dve.wait_ge(x_in[2], 16)
            body(0, False)
            dve.wait_ge(x_in[3], 16)
            with dve.Fori(1, NCH // 2 - 1) as i:
                body(i, False)
            body(NCH // 2 - 1, True)
            dve.wait_ge(ident_ready, 1)
            nc.vector.tensor_copy(identb[:, :], identf[:, :])
            nc.vector.memset(minus1[:, :], -1.0)
            with nc.allow_low_precision(reason="sums of one 1"):
                nc.vector.tensor_reduce(sel[:, :], identf[:, :].rearrange("p (h q) -> p q h", h=HH), X_AXIS, ALU.add)
            nc.vector.memset(hmask[:, :], 0.0).then_inc(tab_ready, 1)
            dve.wait_ge(tab_ready, 5)
            for h in range(HH):
                nc.vector.memset(hmask[32 * h:32 * h + 32, h:h + 1], 1.0)
            nc.vector.memset(v_sb[:, :, :, VD:VD + 1], 1.0)
            nc.vector.memset(gv[:, :, HD:HD + 1], 1.0)
            add_hidden(NCH - 1, bass.ds(TOK // P - CH, CH))

        @block.tensor
        def _(pe):
            def transpose(c, p):
                pe.wait_ge(xn_ready, c + 1)
                wait(pe, xlo_ready, c)
                for t in range(CH):
                    ins = nc.tensor.transpose(ps_t[:, P * t:P * t + P], xn[:, p, t, :], identf[:, :])
                ins.then_inc(xnT_ready, 1)

            pe.wait_ge(ident_ready, 1)
            transpose(0, 0)
            pe.wait_ge(wabs_ready, 1)
            pe.wait_ge(ones_ready, 2)
            nc.tensor.matmul(ps_f[:, 0:2], onesf, wabs[:, :], start=True, stop=True).then_inc(gamma_ready, 1)
            pe.wait_ge(w_in, 144)

            def up(c, p, f):
                wait(pe, hhi_ready, c * FT + f - 1)
                for x in range(2):
                    ins = nc.tensor.matmul(ps_s[:, 0, f % 2, :], w16[:, 0, P * f:P * f + P], xT16[:, p, x, :],
                                           start=(x == 0), stop=(x == 1))
                ins.then_inc(h_ready, 1)

            def down(c):
                wait(pe, y_ready, c)
                for f in range(FT):
                    pe.wait_ge(hlo_ready, c * FT + f + 1)
                    for t in range(CH):
                        for x in range(2):
                            ins = nc.tensor.matmul(ps_f[:, P * t:P * t + P], hid[:, x, f, P * t:P * t + P],
                                                   w16[:, 1, P * f:P * f + P], start=(f == 0 and x == 0 and t == 0),
                                                   stop=False, skip_group_check=True)
                    ins.then_inc(hid_used, 1)
                add_bias(ps_f, 0).then_inc(f_ready, 1)

            def add_bias(bank, which):
                return nc.tensor.matmul(bank.rearrange("p (t n) -> p t n", t=CH), pick[0:64, :],
                                        bhl[0:64, which, :].rearrange("p (o n) -> p o n", o=1).to_broadcast([64, CH, D]),
                                        start=False, stop=True, skip_group_check=True)

            def body(i, last):
                for p in range(2):
                    c = 2 * i + p
                    pe.wait_ge(xT_ready, c + 1)
                    wait(pe, qlo_ready, c)
                    nc.tensor.matmul(ps_o[:, :], wqkv[:, 0, :], xT[:, p, :], start=True, stop=True).then_inc(q_ready, 1)
                    if not (last and p == 1):
                        transpose(c + 1, 1 - p)
                    if isinstance(i, int) and c == 0:
                        pe.wait_ge(wq_ready, 1)
                    pe.wait_ge(xlo_ready, c + 1)
                    up(c, p, 0)
                    up(c, p, 1)
                    if not (isinstance(i, int) and c == 0):
                        down(c - 1)
                    wait(pe, klo_ready, c)
                    nc.tensor.matmul(ps_r[:, :], wqkv[:, 1, :], xT[:, p, :], start=True, stop=True).then_inc(k_ready, 1)
                    up(c, p, 2)
                    up(c, p, 3)
                    wait(pe, v_copied, 2 * c)
                    if isinstance(i, int) and c == 0:
                        pe.wait_ge(bias_ready, 1)
                    for t in range(CH):
                        nc.tensor.matmul(ps_y[:, P * t:P * t + P], xT[:, p, P * t:P * t + P], wqkv[:, 2, :],
                                         start=(t == 0), stop=False, skip_group_check=True)
                    add_bias(ps_y[:, :], 1).then_inc(v_ready, 1)
            loop(pe, body)
            down(NCH - 1)


def build_main(nc, v):
    q_dram, q_out = v["q_dram"], v["q_out"]
    kst, e4, qbd, qrel, v_sb, gv, probs = v["kst"], v["e4"], v["qbd"], v["qrel"], v["v_sb"], v["gv"], v["probs"]
    s0, p32, rsum = v["s0"], v["p32"], v["rsum"]
    attT, xr, mx, mcol, mdiag = v["attT"], v["xr"], v["mx"], v["mcol"], v["mdiag"]
    obd2, gwin, ewin = v["obd2"], v["gwin"], v["ewin"]
    rden, rmask, obd, rrden, hmask, sel = v["rden"], v["rmask"], v["obd"], v["rrden"], v["hmask"], v["sel"]
    identb, minus1 = v["identb"], v["minus1"]
    ps_s, ps_o, ps_r, ps_y = v["ps_s"], v["ps_o"], v["ps_r"], v["ps_y"]
    ps_tb = v["ps_t"][:, 0:COLS // 2].bitcast(BF16).rearrange("p (g n) -> p g n", g=G)
    o_ps = ps_o[:, 0:G * (VD + 1)].rearrange("p (g e) -> p g e", g=G)
    r_ps = ps_r[:, 0:QH * RC].rearrange("p (q e) -> p q e", e=RC)
    y_ps = ps_y[:, 0:8 * QN].rearrange("p (b q) -> p b q", b=8)
    NDMA = 2 * PARTS * 4
    y_dram, out, identf, ps_t = v["y_dram"], v["out"], v["identf"], v["ps_t"]
    OUT_PARTS = [(bg, qh) for qh in range(KH) for bg in range(BG)]
    NT = TOK // P
    y_sb = v["big"][:, 0:NT * D].rearrange("p (t n) -> p t n", n=D)
    y_v, y_src = (t.rearrange("p (b h) d -> p h b d", h=KH) for t in (y_sb, y_dram))
    at = NT * D
    orel = v["big"][:, at:at + 2 * 8 * D].rearrange("p (s b h d) -> p s b h d", s=2, b=8, h=H)
    at += 2 * 8 * D
    oT = v["big"][:, at:at + 2 * 8 * P].rearrange("p (s n) -> p s n", s=2)
    wo_sb = s0[:, :].bitcast(F32)[:, 0:D]
    out_t = out.rearrange("b (h p) d -> h p b d", p=P)
    ALL = NQB * UNITS

    ctx = ExitStack()
    with ctx:
        def sem(name):
            return ctx.enter_context(nc.semaphore(name))

        q_in = v["q_in"]
        half_ready, half_copied = sem("half_ready"), sem("half_copied")
        scores_ready, max_ready, maxT_ready = sem("scores_ready"), sem("max_ready"), sem("maxT_ready")
        mcol_ready, mdiag_ready = sem("mcol_ready"), sem("mdiag_ready")
        shifted0, shifted, exp0_ready, hi0_ready = sem("shifted0"), sem("shifted"), sem("exp0_ready"), sem("hi0_ready")
        hi_ready, lo_ready, pool_lo_ready = sem("hi_ready"), sem("lo_ready"), sem("pool_lo_ready")
        rsum_ready, gwin_ready, ewin_ready = sem("rsum_ready"), sem("gwin_ready"), sem("ewin_ready")
        obd_hi_ready, obd_lo_ready = sem("obd_hi_ready"), sem("obd_lo_ready")
        exp_ready, pv_ready, rden_ready, rmask_ready, obd_ready = sem("exp_ready"), sem("pv_ready"), sem("rden_ready"), sem("rmask_ready"), sem("obd_ready")
        oT_ready, oT_copied = sem("oT_ready"), sem("oT_copied")
        rel_ready, rrden_ready, rel_copied = sem("rel_ready"), sem("rrden_ready"), sem("rel_copied")
        wo_in, d_ready, orel_ready, relT_ready = sem("wo_in"), sem("d_ready"), sem("orel_ready"), sem("relT_ready")
        y_in = [sem(f"y_in{m}") for m in range(len(OUT_PARTS))]
        oT_sum_ready, out_ready, y_sum_ready, y_sum_out = sem("oT_sum_ready"), sem("out_ready"), sem("y_sum_ready"), sem("y_sum_out")
        block = ctx.enter_context(nc.Block())

        def loop(eng, body):
            body(0, False)
            with eng.Fori(1, NQB - 1) as qb:
                body(qb, False)
            body(NQB - 1, True)

        def unit(qb, k):
            if k < 0 and isinstance(qb, int) and qb == 0:
                return None
            return (qb - 1, k + UNITS) if k < 0 else (qb, k)


        @block.sync
        def _(sp):
            save_rest(sp, v, NCH // 2 - 1)
            stack_keys(sp, v, NCH // 2 - 1, v["kst_last"])

            def body(qb, last):
                for bg in range(BG):
                    su = qb * BG + bg
                    if isinstance(qb, int) and qb == 0:
                        if bg == 0:
                            continue
                        sp.wait_ge(q_out[bg], 32)
                    wait(sp, scores_ready, 8 * (su - 1))
                    load_queries(sp, v, qb, bg)
            loop(sp, body)
            sp.wait_ge(max_ready, ALL)
            sp.dma_start(wo_sb, v["woT"]).then_inc(wo_in, 16)
            sp.wait_ge(rel_ready, 4 * NQB - 2)
            for m, (bg, qh) in enumerate(OUT_PARTS):
                sp.dma_start(y_v[:, qh, 8 * bg:8 * bg + 8, :], y_src[:, qh, 8 * bg:8 * bg + 8, :]).then_inc(y_in[m], 16)
            for m, (bg, qh) in enumerate(OUT_PARTS):
                sp.wait_ge(y_sum_ready, 2 * (m + 1))
                sp.dma_start(out_t[qh, :, 8 * bg:8 * bg + 8, :], y_v[:, qh, 8 * bg:8 * bg + 8, :]).then_inc(y_sum_out, 16)
            sp.wait_ge(y_sum_out, 16 * len(OUT_PARTS))

        @block.tensor
        def _(pe):
            def scores(qb, k):
                if k % 8 == 0:
                    pe.wait_ge(q_in[k // 8], (qb + 1) * (16 * NDMA))
                if k == 0:
                    pe.wait_ge(ewin_ready, qb + 1)
                if isinstance(qb, int) and qb == 0 and S * k == (NCH - 2) * CH * P:
                    pe.wait_ge(v["kst_last"], 16 * PARTS * G)
                for kh in range(KH):
                    wait(pe, (exp0_ready, exp_ready)[kh], UNITS * qb + k - 1)
                    bank = ps_s[:, k % 2, kh, :]
                    for g in range(G):
                        rhs = qbd[:, k // 8, g, :, :].rearrange("p h (j b q) -> p (h j) b q", j=J, b=8)[:, :, k % 8, :]
                        nc.tensor.matmul(bank[:, P * g:P * g + P], kst[:, g, S * k + P * kh:S * k + P * kh + P], rhs,
                                         start=(g == 0), stop=False, skip_group_check=True)
                    for q in range(Q0):
                        rhs = qrel[:, k // 8, :, :, :].rearrange("p h j (b q) -> p (h j) b q", b=8)[:, :, k % 8, q]
                        lhsT = ewin[:, P * kh + Q0 - 1 - q:P * kh + Q0 - 1 - q + P]
                        ins = nc.tensor.matmul(bank.rearrange("p (m q) -> p m q", q=Q0)[:, :, q], lhsT, rhs,
                                               start=False, stop=(q == Q0 - 1), skip_group_check=True)
                    ins.then_inc((half_ready, scores_ready)[kh], 1)

            def pv(qb, k):
                n = UNITS * qb + k
                pe.wait_ge(hi_ready, n + 1)
                pe.wait_ge(lo_ready, n + 1)
                pe.wait_ge(pool_lo_ready, n + 1)
                wait(pe, obd_ready, n)
                for g in range(G):
                    for kh in range(KH):
                        hi, lo = (probs[:, k // 8, x, kh, k % 8, P * g:P * g + P] for x in range(2))
                        val = v_sb[:, KH * k + kh, g, :]
                        nc.tensor.matmul(o_ps[:, g, :], hi, val[:, 0:VD + 1], start=(g == 0 and kh == 0), stop=False,
                                         skip_group_check=True)
                        nc.tensor.matmul(o_ps[:, g, 0:VD], hi, val[:, VD + 1:VC], start=False, stop=False,
                                         skip_group_check=True)
                        ins = nc.tensor.matmul(o_ps[:, g, :], lo, val[:, 0:VD + 1], start=False,
                                               stop=(g == G - 1 and kh == KH - 1), skip_group_check=True)
                ins.then_inc(pv_ready, 1)

            def transposed(qb, k):
                pe.wait_ge(obd_lo_ready, UNITS * qb + k + 1)
                if k % 8 == 0:
                    wait(pe, oT_copied, BG * qb + k // 8)
                for x in range(2):
                    ins = nc.tensor.matmul(y_ps[:, k % 8, :], obd2[:, k % 2, x, :, :, :].rearrange("p g h d -> p (g h d)"), sel[:, :],
                                           start=(x == 0), stop=(x == 1))
                ins.then_inc(oT_ready, 1)

            def relative(qb, bg, part):
                first, last = sum(REL_PARTS[:part]), sum(REL_PARTS[:part + 1])
                if first % QH == 0:
                    wait(pe, rsum_ready, 2 * (BG * qb + bg) + first // QH)
                if bg == 0:
                    pe.wait_ge(gwin_ready, QN // 8 * qb + (last - 1) // 8 + 1)
                for q in range(first, last):
                    for kh in range(KH):
                        hi, lo = (probs[:, bg, x, kh, :, :].rearrange("p b (h q) -> p (b h) q", q=QN)[:, :, q] for x in range(2))
                        win = gwin[:, kh, QN - 1 - q, :]
                        nc.tensor.matmul(r_ps[:, q % QH, :], hi, win, start=(q % QH == 0 and kh == 0), stop=False,
                                         skip_group_check=True)
                        ins = nc.tensor.matmul(r_ps[:, q % QH, 0:HD + 1], lo, win[:, 0:HD + 1], start=False,
                                               stop=(q % QH == QH - 1 and kh == KH - 1), skip_group_check=True)
                if last % QH == 0:
                    ins.then_inc(rel_ready, 1)

            def relative_step(qb, k):
                for bg in range(BG):
                    for back in range(2):
                        part = k + UNITS * back - (10 + 8 * bg)
                        if 0 <= part < len(REL_PARTS) and not (back and isinstance(qb, int) and qb == 0):
                            relative(qb - back, bg, part)

            def components_by_query(m):
                bg, qh = OUT_PARTS[m]
                pe.wait_ge(rel_copied, (4 * NQB // KH, 4 * NQB - 2 + 2 * bg)[qh])
                pe.wait_ge(exp_ready, ALL - 1)
                for half in range(2):
                    wait(pe, orel_ready, 2 * (m - 1) + half + 1)
                    for d in range(4):
                        ins = nc.tensor.transpose(ps_s[:, 0, half, P * d:P * d + P],
                                                  xr[:, bg, P * qh:P * qh + P, 4 * half + d], identf[:, :])
                    ins.then_inc(d_ready, 1)

            def relative_by_head(m):
                pe.wait_ge(exp_ready, ALL)
                pe.wait_ge(orel_ready, 2 * (m + 1))
                for half in range(2):
                    wait(pe, oT_sum_ready, 2 * (m - 1) + half + 1)
                    for b in range(4):
                        ins = nc.tensor.transpose(ps_s[:, 1, half, P * b:P * b + P],
                                                  orel[:, m % 2, 4 * half + b, :, :].rearrange("p h d -> p (h d)"), identf[:, :])
                    ins.then_inc(relT_ready, 1)

            def project(m):
                pe.wait_ge(wo_in, 16)
                pe.wait_ge(mcol_ready, ALL)
                pe.wait_ge(obd_ready, ALL)
                for half in range(2):
                    pe.wait_ge(oT_sum_ready, 2 * m + half + 1)
                    wait(pe, y_sum_ready, 2 * (m - 1) + half + 1)
                    for b in range(4):
                        ins = nc.tensor.matmul((ps_t, ps_o)[half][:, P * b:P * b + P],
                                               oT[:, m % 2, P * (4 * half + b):P * (4 * half + b) + P], wo_sb[:, :],
                                               start=True, stop=True)
                    ins.then_inc(out_ready, 1)

            def body(qb, last):
                for k in range(UNITS):
                    n = UNITS * qb + k
                    pe.wait_ge(max_ready, n + 1)
                    wait(pe, mcol_ready, n)
                    for g in range(G):
                        ins = nc.tensor.transpose(ps_tb[:, g, :], mx[:, P * g:P * g + P], identb[:, :])
                    ins.then_inc(maxT_ready, 1)
                    if k < UNITS - 1:
                        scores(qb, k + 1)
                    elif not last:
                        scores(qb + 1, 0)
                    if unit(qb, k - 3):
                        pv(*unit(qb, k - 3))
                    pe.wait_ge(mdiag_ready, n + 1)
                    for kh in range(KH):
                        ins = nc.tensor.matmul(ps_s[:, k % 2, kh, :], minus1[:, :], mdiag[:, :, :].rearrange("p g n -> p (g n)"),
                                               start=False, stop=True, skip_group_check=True)
                        ins.then_inc((shifted0, shifted)[kh], 1)
                    if unit(qb, k - 5):
                        transposed(*unit(qb, k - 5))
                    relative_step(qb, k)
            pe.wait_ge(v["kst_in"], 16 * PARTS * G * (NCH // 2 - 1))
            scores(0, 0)
            loop(pe, body)
            transposed(NQB - 1, UNITS - 5)
            transposed(NQB - 1, UNITS - 4)
            pv(NQB - 1, UNITS - 3)
            relative(NQB - 1, 0, len(REL_PARTS) - 1)
            components_by_query(0)
            transposed(NQB - 1, UNITS - 3)
            pv(NQB - 1, UNITS - 2)
            relative_by_head(0)
            components_by_query(1)
            transposed(NQB - 1, UNITS - 2)
            pv(NQB - 1, UNITS - 1)
            relative_by_head(1)
            for part in range(len(REL_PARTS)):
                if sum(REL_PARTS[:part]) == QH:
                    project(0)
                    transposed(NQB - 1, UNITS - 1)
                relative(NQB - 1, 1, part)
            components_by_query(2)
            project(1)
            relative_by_head(2)
            components_by_query(3)
            project(2)
            relative_by_head(3)
            project(3)

        @block.scalar
        def _(act):
            def copy_oT(qb, bg):
                act.wait_ge(oT_ready, 8 * (BG * qb + bg + 1))
                nc.scalar.activation(attT[:, 8 * bg:8 * bg + 8, bass.ds(qb * QN, QN)], y_ps[:, :, :],
                                     ACT.Copy).then_inc(oT_copied, 1)

            def copy_half(qb, k):
                n = UNITS * qb + k
                act.wait_ge(half_ready, n + 1)
                wait(act, max_ready, n)
                nc.scalar.activation(s0[:, :], ps_s[:, k % 2, 0, :], ACT.Copy).then_inc(half_copied, 1)

            def exponentials(qb, k):
                n = UNITS * qb + k
                act.wait_ge(shifted0, n + 1)
                wait(act, lo_ready, n - 1)
                wait(act, pool_lo_ready, n - 1)
                nc.scalar.activation(p32[:, k % 2, 0, :], ps_s[:, k % 2, 0, :], ACT.Exp, scale=SCALE).then_inc(exp0_ready, 1)
                act.wait_ge(shifted, n + 1)
                nc.scalar.activation(p32[:, k % 2, 1, :], ps_s[:, k % 2, 1, :], ACT.Exp, scale=SCALE).then_inc(exp_ready, 1)

            def high_part(qb, k, kh):
                n = UNITS * qb + k
                if kh == 0:
                    act.wait_ge(exp0_ready, n + 1)
                    if k % 8 == 0:
                        wait(act, rel_ready, 2 * (BG * qb + k // 8 - 1))
                    if isinstance(qb, int) and qb == 0 and k == 0:
                        act.wait_ge(q_out[1], 32)
                        act.wait_ge(v["y_out"], 16 * (NCH // 2))
                    if isinstance(qb, int) and qb == 0 and k == 8:
                        act.wait_ge(v["kst_last"], 16 * PARTS * G)
                else:
                    act.wait_ge(exp_ready, n + 1)
                nc.scalar.activation(probs[:, k // 8, 0, kh, k % 8, :], p32[:, k % 2, kh, :],
                                     ACT.Copy).then_inc((hi0_ready, hi_ready)[kh], 1)

            def high_outputs(qb, k):
                n = UNITS * qb + k
                act.wait_ge(obd_ready, n + 1)
                wait(act, oT_ready, n - 1)
                nc.scalar.activation(obd2[:, k % 2, 0, :, :, :], obd[:, k % 2, :, :, :], ACT.Copy).then_inc(obd_hi_ready, 1)

            def body(qb, last):
                for k in range(UNITS):
                    if unit(qb, k - 1):
                        exponentials(*unit(qb, k - 1))
                    if unit(qb, k - 5):
                        high_outputs(*unit(qb, k - 5))
                    if k == 13:
                        copy_oT(qb, 0)
                    if k == 5 and unit(qb, -1):
                        copy_oT(qb - 1, 1)
                    if unit(qb, k - 1):
                        high_part(*unit(qb, k - 1), 0)
                    if k < UNITS - 1:
                        copy_half(qb, k + 1)
                    elif not last:
                        copy_half(qb + 1, 0)
                    if unit(qb, k - 1):
                        high_part(*unit(qb, k - 1), 1)
                    if k == UNITS - 2 and not last:
                        act.wait_ge(scores_ready, UNITS * (qb + 1))
                        rel_k_window(qb + 1)
                    if 9 <= k < 9 + QN // 8:
                        piece = k - 9
                        if piece == 0 and unit(qb, -1):
                            act.wait_ge(rel_ready, 4 * qb)
                        first = QN - 8 - 8 * piece
                        for kh in range(KH):
                            win = gv[:, bass.ds(qb * -QN + (P * kh + S - QN + first), 8), :]
                            ins = nc.scalar.activation(gwin[:, kh, first:first + 8, :], win, ACT.Copy)
                        ins.then_inc(gwin_ready, 1)

            def rel_k_window(qb):
                nc.scalar.activation(ewin[:, :], e4[:, bass.ds(qb * -QN + (ESTART - Q0 + 1), EWIN)], ACT.Copy).then_inc(ewin_ready, 1)

            rel_k_window(0)
            copy_half(0, 0)
            loop(act, body)

            def components_together(m):
                for half in range(2):
                    act.wait_ge(d_ready, 2 * m + half + 1)
                    wait(act, relT_ready, 2 * (m - 1))
                    nc.scalar.activation(orel[:, m % 2, :, :, 4 * half:4 * half + 4],
                                         ps_s[:, 0, half, :].rearrange("p (d b h) -> p b h d", d=4, b=8),
                                         ACT.Copy).then_inc(orel_ready, 1)

            exponentials(NQB - 1, UNITS - 1)
            high_outputs(NQB - 1, UNITS - 5)
            high_outputs(NQB - 1, UNITS - 4)
            high_part(NQB - 1, UNITS - 1, 0)
            high_part(NQB - 1, UNITS - 1, 1)
            high_outputs(NQB - 1, UNITS - 3)
            components_together(0)
            high_outputs(NQB - 1, UNITS - 2)
            components_together(1)
            high_outputs(NQB - 1, UNITS - 1)
            copy_oT(NQB - 1, 1)
            components_together(2)
            components_together(3)

        def low_part(engine, k, kh, c0, c1):
            return engine.tensor_tensor(probs[:, k // 8, 1, kh, k % 8, c0:c1], p32[:, k % 2, kh, c0:c1],
                                        probs[:, k // 8, 0, kh, k % 8, c0:c1], ALU.subtract)

        @block.gpsimd
        def _(pool):
            def low_outputs(qb, k):
                pool.wait_ge(obd_hi_ready, UNITS * qb + k + 1)
                nc.gpsimd.tensor_tensor(obd2[:, k % 2, 1, :, :, :], obd[:, k % 2, :, :, :], obd2[:, k % 2, 0, :, :, :],
                                        ALU.subtract).then_inc(obd_lo_ready, 1)

            def low_parts(qb, k):
                pool.wait_ge(hi0_ready, UNITS * qb + k + 1)
                low_part(nc.gpsimd, k, 0, LO, COLS)
                pool.wait_ge(hi_ready, UNITS * qb + k + 1)
                low_part(nc.gpsimd, k, 1, 0, COLS).then_inc(pool_lo_ready, 1)

            def body(qb, last):
                for k in range(UNITS):
                    if unit(qb, k - 5):
                        low_outputs(*unit(qb, k - 5))
                    if unit(qb, k - 1):
                        low_parts(*unit(qb, k - 1))
            loop(pool, body)
            low_outputs(NQB - 1, UNITS - 5)
            low_outputs(NQB - 1, UNITS - 4)
            low_parts(NQB - 1, UNITS - 1)
            for k in range(UNITS - 3, UNITS):
                low_outputs(NQB - 1, k)

        @block.vector
        def _(dve):
            def maximum(qb, k):
                n = UNITS * qb + k
                dve.wait_ge(half_copied, n + 1)
                dve.wait_ge(scores_ready, n + 1)
                nc.vector.tensor_tensor(mx[:, :], s0[:, :], ps_s[:, k % 2, 1, :], ALU.max).then_inc(max_ready, 1)

            def low_parts(qb, k):
                dve.wait_ge(hi0_ready, UNITS * qb + k + 1)
                low_part(nc.vector, k, 0, 0, LO).then_inc(lo_ready, 1)

            def denominators(qb, k):
                dve.wait_ge(pv_ready, UNITS * qb + k + 1)
                nc.vector.reciprocal(rden[:, :], o_ps[:, :, VD]).then_inc(rden_ready, 1)

            def denominators_by_head(qb, k):
                dve.wait_ge(rden_ready, UNITS * qb + k + 1)
                nc.vector.tensor_tensor(rmask[:, :, :], rden[:, :].rearrange("p (g o) -> p g o", o=1).to_broadcast([P, G, HH]),
                                        hmask[:, :].rearrange("p (o h) -> p o h", o=1).to_broadcast([P, G, HH]),
                                        ALU.mult).then_inc(rmask_ready, 1)

            def mask_outputs(qb, k):
                n = UNITS * qb + k
                dve.wait_ge(rmask_ready, n + 1)
                wait(dve, obd_lo_ready, n - 1)
                nc.vector.tensor_tensor(obd[:, k % 2, :, :, :], o_ps[:, :, 0:VD].rearrange("p g (h d) -> p g h d", h=HH),
                                        rmask[:, :, :].rearrange("p g (h o) -> p g h o", o=1).to_broadcast([P, G, HH, HD]),
                                        ALU.mult).then_inc(obd_ready, 1)

            def sum_relative(qb, bg, half):
                done = 2 * (BG * qb + bg) + half + 1
                dve.wait_ge(rel_ready, done)
                dve.wait_ge(rel_copied, done - 1)
                nc.vector.reciprocal(rrden[:, :], r_ps[:, :, HD]).then_inc(rrden_ready, 1)
                pairs = bass.AP(tensor=r_ps.tensor, offset=r_ps.offset,
                                ap=[list(r_ps.ap[0]), [RC, QH], [1, HD], [HD + 1, 2]])
                nc.vector.tensor_reduce(rsum[:, :, :], pairs, X_AXIS, ALU.add).then_inc(rsum_ready, 1)

            def divide_relative(qb, bg, half):
                done = 2 * (BG * qb + bg) + half + 1
                dve.wait_ge(rrden_ready, done)
                dve.wait_ge(rsum_ready, done)
                nc.vector.tensor_tensor(xr[:, bg, bass.ds(qb * QN + QH * half, QH), :], rsum[:, :, :],
                                        rrden[:, :].rearrange("p (q o) -> p q o", o=1).to_broadcast([P, QH, HD]),
                                        ALU.mult).then_inc(rel_copied, 1)

            def relative_of(qb, k):
                for bg in range(BG):
                    for half in range(2):
                        at = 14 + 8 * bg + 3 * half
                        if k == at % UNITS and (at < UNITS or unit(qb, -1)):
                            return qb - at // UNITS, bg, half

            def body(qb, last):
                for k in range(UNITS):
                    n = UNITS * qb + k
                    dve.wait_ge(maxT_ready, n + 1)
                    nc.vector.tensor_reduce(mcol[:, k % 2, :], ps_tb, X_AXIS, ALU.max).then_inc(mcol_ready, 1)
                    if unit(qb, k - 4):
                        mask_outputs(*unit(qb, k - 4))
                    dve.wait_ge(mcol_ready, n + 1)
                    wait(dve, shifted, n)
                    nc.vector.tensor_tensor(mdiag[:, :, :], identb[:, :].rearrange("p (o n) -> p o n", o=1).to_broadcast([P, G, P]),
                                            mcol[:, k % 2, :].rearrange("p (g o) -> p g o", o=1).to_broadcast([P, G, P]),
                                            ALU.mult).then_inc(mdiag_ready, 1)
                    rel = relative_of(qb, k)
                    if rel:
                        sum_relative(*rel)
                    if k < UNITS - 1:
                        maximum(qb, k + 1)
                    elif not last:
                        maximum(qb + 1, 0)
                    if unit(qb, k - 3):
                        denominators(*unit(qb, k - 3))
                    if unit(qb, k - 1):
                        low_parts(*unit(qb, k - 1))
                    if unit(qb, k - 3):
                        denominators_by_head(*unit(qb, k - 3))
                    rel = relative_of(qb, k - 1) if k else None
                    if rel:
                        divide_relative(*rel)
            maximum(0, 0)
            loop(dve, body)

            def outputs(k):
                denominators(NQB - 1, k)
                denominators_by_head(NQB - 1, k)
                mask_outputs(NQB - 1, k)

            def sum_terms(m):
                bg, qh = OUT_PARTS[m]
                dve.wait_ge(oT_copied, (BG * NQB // KH, BG * NQB - 1 + bg)[qh])
                for half in range(2):
                    dve.wait_ge(relT_ready, 2 * m + half + 1)
                    wait(dve, out_ready, 2 * (m - 1))
                    b0 = 8 * bg + 4 * half
                    nc.vector.tensor_tensor(oT[:, m % 2, 4 * P * half:4 * P * half + 4 * P].rearrange("p (b q) -> p b q", b=4),
                                            ps_s[:, 1, half, :].rearrange("p (b q) -> p b q", b=4),
                                            attT[:, b0:b0 + 4, P * qh:P * qh + P], ALU.add).then_inc(oT_sum_ready, 1)

            def add_rest(m):
                bg, qh = OUT_PARTS[m]
                dve.wait_ge(y_in[m], 16)
                for half in range(2):
                    dve.wait_ge(out_ready, 2 * m + half + 1)
                    b0 = 8 * bg + 4 * half
                    nc.vector.tensor_tensor(y_v[:, qh, b0:b0 + 4, :], (ps_t, ps_o)[half][:, :].rearrange("p (b n) -> p b n", b=4),
                                            y_v[:, qh, b0:b0 + 4, :], ALU.add).then_inc(y_sum_ready, 1)

            mask_outputs(NQB - 1, UNITS - 4)
            outputs(UNITS - 3)
            low_parts(NQB - 1, UNITS - 1)
            sum_relative(NQB - 1, 0, 1)
            divide_relative(NQB - 1, 0, 1)
            outputs(UNITS - 2)
            sum_terms(0)
            outputs(UNITS - 1)
            sum_terms(1)
            sum_relative(NQB - 1, 1, 0)
            divide_relative(NQB - 1, 1, 0)
            add_rest(0)
            sum_relative(NQB - 1, 1, 1)
            divide_relative(NQB - 1, 1, 1)
            add_rest(1)
            sum_terms(2)
            add_rest(2)
            sum_terms(3)
            add_rest(3)


def kernel(**inputs):
    import concourse.bacc as bacc
    from concourse.bass_utils import run_bass_kernel_spmd

    names = {"L0_attn_x": "x", "L0_attn_Wq": "wqT", "L0_attn_bq": "bq", "L0_attn_Wk": "wkT", "L0_attn_bk": "bk",
             "L0_attn_Wv": "wvT", "L0_attn_bv": "bv", "L0_attn_Wo": "woT", "L0_attn_bo": "bo",
             "L0_attn_rel_k": "rel_kT", "L0_attn_rel_v": "rel_v", "L0_ffn_W1": "w1T", "L0_ffn_b1": "b1",
             "L0_ffn_W2": "w2T", "L0_ffn_b2": "b2"}
    nc = bacc.Bacc("TRN2", target_bir_lowering=False, num_devices=1)
    arrays, args = {}, {}
    for name, short in names.items():
        a = np.asarray(inputs[name])
        a = np.ascontiguousarray(a.T if short.endswith("T") else a)
        arrays[f"in_{short}"] = a
        args[short] = nc.dram_tensor(f"in_{short}", a.shape, mybir.dt.from_np(a.dtype), kind="ExternalInput").ap()
    out = nc.dram_tensor("out", (B, S, D), F32, kind="ExternalOutput").ap()
    layer_kernel(nc, out=out, **args)
    r = run_bass_kernel_spmd(nc, [arrays], core_ids=[0])
    return r.results[0]["out"]
```
